# Optimizing a Trainium2 kernel written in Bass

```python
import numpy as np
import jax
import jax.numpy as jnp

def _softmax(x, axis=-1):
    return jax.nn.softmax(x, axis=axis)

def _gelu(x):
    return jax.nn.gelu(x, approximate=True)

def _silu(x):
    return jax.nn.silu(x)

def _sigmoid(x):
    return jax.nn.sigmoid(x)

def _layernorm(x, axis=-1, eps=1e-05):
    m = jnp.mean(x, axis=axis, keepdims=True)
    v = jnp.var(x, axis=axis, keepdims=True)
    return (x - m) / jnp.sqrt(v + eps)

def _scatter_add(tgt, idx, src, axis=0):
    return tgt.at[idx].add(src)

def _segment_sum(src, seg, n):
    return jax.ops.segment_sum(src, seg, n)
kernel_name = 'mk_conv_preact_d2_conv_nchw128_r4_cb332c'

def setup_inputs(seed: int=0):
    np.random.seed(seed)
    _w = jnp.asarray

    def _rec_inputs():
        import jax
        import jax.numpy as jnp
        _gk = jax.random.key(seed)
        x = -0.0002023 + 1 * jax.random.normal(jax.random.fold_in(_gk, 1), (1, 32, 56, 56), jnp.float32)
        return x
    x = _rec_inputs()

    def _L0_conv_setup():
        import jax, jax.numpy as jnp
        import numpy as np
        NUM_HEAD = 4
        PATCH = (7, 7)
        GRID = (7, 7)

        def rel_pos_index(wh, ww):
            coords = np.stack(np.meshgrid(np.arange(wh), np.arange(ww), indexing='ij'))
            flat = coords.reshape(2, -1)
            rel = flat[:, :, None] - flat[:, None, :]
            rel = np.transpose(rel, (1, 2, 0)).astype(np.int64)
            rel[..., 0] += wh - 1
            rel[..., 1] += ww - 1
            rel[..., 0] *= 2 * ww - 1
            return jnp.asarray(rel.sum(-1))

        def window_partition(x, wh, ww):
            B, C, H, W = x.shape
            x = x.reshape(B, C, H // wh, wh, W // ww, ww).transpose(0, 2, 4, 3, 5, 1)
            return x.reshape(-1, wh, ww, C)

        def unbind_win(x, wh, ww, H, W):
            C = x.shape[-1]
            x = x.reshape(-1, H // wh, W // ww, wh, ww, C).transpose(0, 5, 1, 3, 4, 2)
            return x.reshape(-1, H, W, C)

        def layernorm(x, g, b, eps=1e-05):
            mu = x.mean(-1, keepdims=True)
            var = ((x - mu) ** 2).mean(-1, keepdims=True)
            return (x - mu) * jax.lax.rsqrt(var + eps) * g + b

        def mha(x, qkv_w, proj_w, proj_b, rel_table, rel_idx):
            B, N, D = x.shape
            hd = D // NUM_HEAD
            qkv = (x @ qkv_w.T).reshape(B, N, 3, NUM_HEAD, hd).transpose(2, 0, 3, 1, 4)
            q, k, v = (qkv[0], qkv[1], qkv[2])
            attn = jnp.einsum('bhnd,bhmd->bhnm', q, k) * hd ** 0.5
            bias = rel_table[rel_idx.reshape(-1)].reshape(N, N, NUM_HEAD).transpose(2, 0, 1)
            attn = jax.nn.softmax(attn + bias[None], axis=-1)
            out = jnp.einsum('bhnm,bhmd->bhnd', attn, v).transpose(0, 2, 1, 3).reshape(B, N, D)
            return out @ proj_w.T + proj_b

        def tblock(x, rel_table, rel_idx, qkv_w, proj_w, proj_b, ln_g, ln_b, fc1_w, fc1_b, fc2_w, fc2_b):
            net = mha(x, qkv_w, proj_w, proj_b, rel_table, rel_idx) + x
            net = layernorm(net, ln_g, ln_b)
            shortcut = net
            net = net @ fc1_w.T + fc1_b
            net = net @ fc2_w.T + fc2_b
            return net + shortcut

        def _forward(x, b_rel_table, b_qkv_w, b_proj_w, b_proj_b, b_ln_g, b_ln_b, b_fc1_w, b_fc1_b, b_fc2_w, b_fc2_b, g_rel_table, g_qkv_w, g_proj_w, g_proj_b, g_ln_g, g_ln_b, g_fc1_w, g_fc1_b, g_fc2_w, g_fc2_b):
            H, W = (x.shape[2], x.shape[3])
            ph, pw = PATCH
            gh, gw = (H // GRID[0], W // GRID[1])
            idx_b = rel_pos_index(ph, pw)
            idx_g = rel_pos_index(gh, gw)
            net = window_partition(x, ph, pw)
            nb, h, w, ch = net.shape
            net = tblock(net.reshape(nb, h * w, ch), b_rel_table, idx_b, b_qkv_w, b_proj_w, b_proj_b, b_ln_g, b_ln_b, b_fc1_w, b_fc1_b, b_fc2_w, b_fc2_b)
            net = unbind_win(net.reshape(nb, h, w, ch), ph, pw, H, W).transpose(0, 3, 1, 2)
            net = window_partition(net, gh, gw)
            nb, h, w, ch = net.shape
            net = tblock(net.reshape(nb, h * w, ch), g_rel_table, idx_g, g_qkv_w, g_proj_w, g_proj_b, g_ln_g, g_ln_b, g_fc1_w, g_fc1_b, g_fc2_w, g_fc2_b)
            net = unbind_win(net.reshape(nb, h, w, ch), gh, gw, H, W).transpose(0, 3, 1, 2)
            return net
        key = jax.random.key(seed)
        ks = jax.random.split(key, 24)
        C, E = (32, 128)

        def rn(k, shape, s=0.05):
            return jax.random.normal(k, shape, dtype=jnp.float32) * s
        inp = {'x': rn(ks[0], (1, C, 56, 56), 1.0)}
        for i, p in enumerate(['b', 'g']):
            tbl = (2 * 7 - 1) ** 2 if p == 'b' else (2 * 32 - 1) ** 2
            o = i * 5
            inp[p + '_rel_table'] = rn(ks[1 + o], (tbl, NUM_HEAD), 0.02)
            inp[p + '_qkv_w'] = rn(ks[2 + o], (3 * C, C))
            inp[p + '_proj_w'] = rn(ks[3 + o], (C, C))
            inp[p + '_proj_b'] = jnp.zeros((C,), jnp.float32)
            inp[p + '_ln_g'] = jnp.ones((C,), jnp.float32)
            inp[p + '_ln_b'] = jnp.zeros((C,), jnp.float32)
            inp[p + '_fc1_w'] = rn(ks[4 + o], (E, C))
            inp[p + '_fc1_b'] = jnp.zeros((E,), jnp.float32)
            inp[p + '_fc2_w'] = rn(ks[5 + o], (C, E))
            inp[p + '_fc2_b'] = jnp.zeros((C,), jnp.float32)
        return inp
    _L0_conv_all = _L0_conv_setup()
    _L0_conv_in = {k: v for k, v in _L0_conv_all.items() if k in ('b_rel_table', 'b_qkv_w', 'b_proj_w', 'b_proj_b', 'b_ln_g', 'b_ln_b', 'b_fc1_w', 'b_fc1_b', 'b_fc2_w', 'b_fc2_b', 'g_rel_table', 'g_qkv_w', 'g_proj_w', 'g_proj_b', 'g_ln_g', 'g_ln_b', 'g_fc1_w', 'g_fc1_b', 'g_fc2_w', 'g_fc2_b')}
    del _L0_conv_all

    def _L1_conv_setup():
        import jax, jax.numpy as jnp
        import numpy as np
        import math
        BATCH, SEQ, HH, WW = (32, 32, 32, 32)
        D_MODEL = 256
        N2 = 4
        L_MAX = 16

        def _layernorm(x, gamma, beta, eps=1e-05):
            mu = jnp.mean(x, axis=-1, keepdims=True)
            var = jnp.var(x, axis=-1, keepdims=True)
            return (x - mu) * jax.lax.rsqrt(var + eps) * gamma + beta
        key = jax.random.key(seed)
        ks = jax.random.split(key, 12)
        d_in = SEQ
        inp = {'x': jax.random.normal(ks[0], (BATCH, SEQ, HH, WW), dtype=jnp.float32), 'W_enc': jax.random.normal(ks[1], (d_in, D_MODEL), dtype=jnp.float32) / math.sqrt(d_in), 'b_enc': jnp.zeros((D_MODEL,), dtype=jnp.float32), 'log_dt': jax.random.uniform(ks[2], (D_MODEL,), dtype=jnp.float32) * (math.log(0.1) - math.log(0.001)) + math.log(0.001), 'A_log_real': jnp.full((D_MODEL, N2), math.log(0.5), dtype=jnp.float32), 'A_imag': jnp.broadcast_to(math.pi * jnp.arange(N2, dtype=jnp.float32), (D_MODEL, N2)).copy(), 'C_real': jax.random.normal(ks[3], (D_MODEL, N2), dtype=jnp.float32) * 0.5, 'C_imag': jax.random.normal(ks[4], (D_MODEL, N2), dtype=jnp.float32) * 0.5, 'D': jax.random.normal(ks[5], (D_MODEL,), dtype=jnp.float32), 'W_glu': jax.random.normal(ks[6], (D_MODEL, 2 * D_MODEL), dtype=jnp.float32) / math.sqrt(D_MODEL), 'b_glu': jnp.zeros((2 * D_MODEL,), dtype=jnp.float32), 'ln_gamma': jnp.ones((D_MODEL,), dtype=jnp.float32), 'ln_beta': jnp.zeros((D_MODEL,), dtype=jnp.float32), 'W_dec': jax.random.normal(ks[7], (D_MODEL, d_in), dtype=jnp.float32) / math.sqrt(D_MODEL), 'b_dec': jnp.zeros((d_in,), dtype=jnp.float32)}
        return inp
    _L1_conv_all = _L1_conv_setup()
    _L1_conv_in = {k: v for k, v in _L1_conv_all.items() if k in ('W_enc', 'b_enc', 'log_dt', 'A_log_real', 'A_imag', 'C_real', 'C_imag', 'D', 'W_glu', 'b_glu', 'ln_gamma', 'ln_beta', 'W_dec', 'b_dec')}
    del _L1_conv_all
    return {'x': x, 'L0_conv_b_rel_table': _L0_conv_in['b_rel_table'], 'L0_conv_b_qkv_w': _L0_conv_in['b_qkv_w'], 'L0_conv_b_proj_w': _L0_conv_in['b_proj_w'], 'L0_conv_b_proj_b': _L0_conv_in['b_proj_b'], 'L0_conv_b_ln_g': _L0_conv_in['b_ln_g'], 'L0_conv_b_ln_b': _L0_conv_in['b_ln_b'], 'L0_conv_b_fc1_w': _L0_conv_in['b_fc1_w'], 'L0_conv_b_fc1_b': _L0_conv_in['b_fc1_b'], 'L0_conv_b_fc2_w': _L0_conv_in['b_fc2_w'], 'L0_conv_b_fc2_b': _L0_conv_in['b_fc2_b'], 'L0_conv_g_rel_table': _L0_conv_in['g_rel_table'], 'L0_conv_g_qkv_w': _L0_conv_in['g_qkv_w'], 'L0_conv_g_proj_w': _L0_conv_in['g_proj_w'], 'L0_conv_g_proj_b': _L0_conv_in['g_proj_b'], 'L0_conv_g_ln_g': _L0_conv_in['g_ln_g'], 'L0_conv_g_ln_b': _L0_conv_in['g_ln_b'], 'L0_conv_g_fc1_w': _L0_conv_in['g_fc1_w'], 'L0_conv_g_fc1_b': _L0_conv_in['g_fc1_b'], 'L0_conv_g_fc2_w': _L0_conv_in['g_fc2_w'], 'L0_conv_g_fc2_b': _L0_conv_in['g_fc2_b'], 'L1_conv_W_enc': _L1_conv_in['W_enc'], 'L1_conv_b_enc': _L1_conv_in['b_enc'], 'L1_conv_log_dt': _L1_conv_in['log_dt'], 'L1_conv_A_log_real': _L1_conv_in['A_log_real'], 'L1_conv_A_imag': _L1_conv_in['A_imag'], 'L1_conv_C_real': _L1_conv_in['C_real'], 'L1_conv_C_imag': _L1_conv_in['C_imag'], 'L1_conv_D': _L1_conv_in['D'], 'L1_conv_W_glu': _L1_conv_in['W_glu'], 'L1_conv_b_glu': _L1_conv_in['b_glu'], 'L1_conv_ln_gamma': _L1_conv_in['ln_gamma'], 'L1_conv_ln_beta': _L1_conv_in['ln_beta'], 'L1_conv_W_dec': _L1_conv_in['W_dec'], 'L1_conv_b_dec': _L1_conv_in['b_dec']}

def reference(x, L0_conv_b_rel_table, L0_conv_b_qkv_w, L0_conv_b_proj_w, L0_conv_b_proj_b, L0_conv_b_ln_g, L0_conv_b_ln_b, L0_conv_b_fc1_w, L0_conv_b_fc1_b, L0_conv_b_fc2_w, L0_conv_b_fc2_b, L0_conv_g_rel_table, L0_conv_g_qkv_w, L0_conv_g_proj_w, L0_conv_g_proj_b, L0_conv_g_ln_g, L0_conv_g_ln_b, L0_conv_g_fc1_w, L0_conv_g_fc1_b, L0_conv_g_fc2_w, L0_conv_g_fc2_b, L1_conv_W_enc, L1_conv_b_enc, L1_conv_log_dt, L1_conv_A_log_real, L1_conv_A_imag, L1_conv_C_real, L1_conv_C_imag, L1_conv_D, L1_conv_W_glu, L1_conv_b_glu, L1_conv_ln_gamma, L1_conv_ln_beta, L1_conv_W_dec, L1_conv_b_dec):
    import jax
    import jax.numpy as jnp

    def _L0_conv_ref(x, b_rel_table, b_qkv_w, b_proj_w, b_proj_b, b_ln_g, b_ln_b, b_fc1_w, b_fc1_b, b_fc2_w, b_fc2_b, g_rel_table, g_qkv_w, g_proj_w, g_proj_b, g_ln_g, g_ln_b, g_fc1_w, g_fc1_b, g_fc2_w, g_fc2_b):
        import jax, jax.numpy as jnp
        import numpy as np
        NUM_HEAD = 4
        PATCH = (7, 7)
        GRID = (7, 7)

        def rel_pos_index(wh, ww):
            coords = np.stack(np.meshgrid(np.arange(wh), np.arange(ww), indexing='ij'))
            flat = coords.reshape(2, -1)
            rel = flat[:, :, None] - flat[:, None, :]
            rel = np.transpose(rel, (1, 2, 0)).astype(np.int64)
            rel[..., 0] += wh - 1
            rel[..., 1] += ww - 1
            rel[..., 0] *= 2 * ww - 1
            return jnp.asarray(rel.sum(-1))

        def window_partition(x, wh, ww):
            B, C, H, W = x.shape
            x = x.reshape(B, C, H // wh, wh, W // ww, ww).transpose(0, 2, 4, 3, 5, 1)
            return x.reshape(-1, wh, ww, C)

        def unbind_win(x, wh, ww, H, W):
            C = x.shape[-1]
            x = x.reshape(-1, H // wh, W // ww, wh, ww, C).transpose(0, 5, 1, 3, 4, 2)
            return x.reshape(-1, H, W, C)

        def layernorm(x, g, b, eps=1e-05):
            mu = x.mean(-1, keepdims=True)
            var = ((x - mu) ** 2).mean(-1, keepdims=True)
            return (x - mu) * jax.lax.rsqrt(var + eps) * g + b

        def mha(x, qkv_w, proj_w, proj_b, rel_table, rel_idx):
            B, N, D = x.shape
            hd = D // NUM_HEAD
            qkv = (x @ qkv_w.T).reshape(B, N, 3, NUM_HEAD, hd).transpose(2, 0, 3, 1, 4)
            q, k, v = (qkv[0], qkv[1], qkv[2])
            attn = jnp.einsum('bhnd,bhmd->bhnm', q, k) * hd ** 0.5
            bias = rel_table[rel_idx.reshape(-1)].reshape(N, N, NUM_HEAD).transpose(2, 0, 1)
            attn = jax.nn.softmax(attn + bias[None], axis=-1)
            out = jnp.einsum('bhnm,bhmd->bhnd', attn, v).transpose(0, 2, 1, 3).reshape(B, N, D)
            return out @ proj_w.T + proj_b

        def tblock(x, rel_table, rel_idx, qkv_w, proj_w, proj_b, ln_g, ln_b, fc1_w, fc1_b, fc2_w, fc2_b):
            net = mha(x, qkv_w, proj_w, proj_b, rel_table, rel_idx) + x
            net = layernorm(net, ln_g, ln_b)
            shortcut = net
            net = net @ fc1_w.T + fc1_b
            net = net @ fc2_w.T + fc2_b
            return net + shortcut

        def _forward(x, b_rel_table, b_qkv_w, b_proj_w, b_proj_b, b_ln_g, b_ln_b, b_fc1_w, b_fc1_b, b_fc2_w, b_fc2_b, g_rel_table, g_qkv_w, g_proj_w, g_proj_b, g_ln_g, g_ln_b, g_fc1_w, g_fc1_b, g_fc2_w, g_fc2_b):
            H, W = (x.shape[2], x.shape[3])
            ph, pw = PATCH
            gh, gw = (H // GRID[0], W // GRID[1])
            idx_b = rel_pos_index(ph, pw)
            idx_g = rel_pos_index(gh, gw)
            net = window_partition(x, ph, pw)
            nb, h, w, ch = net.shape
            net = tblock(net.reshape(nb, h * w, ch), b_rel_table, idx_b, b_qkv_w, b_proj_w, b_proj_b, b_ln_g, b_ln_b, b_fc1_w, b_fc1_b, b_fc2_w, b_fc2_b)
            net = unbind_win(net.reshape(nb, h, w, ch), ph, pw, H, W).transpose(0, 3, 1, 2)
            net = window_partition(net, gh, gw)
            nb, h, w, ch = net.shape
            net = tblock(net.reshape(nb, h * w, ch), g_rel_table, idx_g, g_qkv_w, g_proj_w, g_proj_b, g_ln_g, g_ln_b, g_fc1_w, g_fc1_b, g_fc2_w, g_fc2_b)
            net = unbind_win(net.reshape(nb, h, w, ch), gh, gw, H, W).transpose(0, 3, 1, 2)
            return net
        return _forward(x, b_rel_table, b_qkv_w, b_proj_w, b_proj_b, b_ln_g, b_ln_b, b_fc1_w, b_fc1_b, b_fc2_w, b_fc2_b, g_rel_table, g_qkv_w, g_proj_w, g_proj_b, g_ln_g, g_ln_b, g_fc1_w, g_fc1_b, g_fc2_w, g_fc2_b)

    def _L1_conv_ref(x, W_enc, b_enc, log_dt, A_log_real, A_imag, C_real, C_imag, D, W_glu, b_glu, ln_gamma, ln_beta, W_dec, b_dec):
        import jax, jax.numpy as jnp
        import numpy as np
        import math
        BATCH, SEQ, HH, WW = (32, 32, 32, 32)
        D_MODEL = 256
        N2 = 4
        L_MAX = 16

        def _layernorm(x, gamma, beta, eps=1e-05):
            mu = jnp.mean(x, axis=-1, keepdims=True)
            var = jnp.var(x, axis=-1, keepdims=True)
            return (x - mu) * jax.lax.rsqrt(var + eps) * gamma + beta
        Bsz, S, Hh, Ww = x.shape
        L = Hh * Ww
        u = x.reshape(Bsz, S, L)
        h = jnp.einsum('bdl,de->ble', u, W_enc) + b_enc
        dt = jnp.exp(log_dt)
        A = -jnp.exp(A_log_real) + 1j * A_imag
        Cc = C_real + 1j * C_imag
        dtA = A * dt[:, None]
        Bd = (jnp.exp(dtA) - 1.0) / A
        t = jnp.arange(L_MAX)
        vand = jnp.exp(dtA[:, :, None] * t)
        K = 2.0 * jnp.einsum('dn,dnl->dl', Cc * Bd, vand).real
        z = jnp.swapaxes(h, 1, 2)
        n_fft = L + L_MAX
        y = jnp.fft.irfft(jnp.fft.rfft(z, n=n_fft) * jnp.fft.rfft(K, n=n_fft), n=n_fft)[..., :L]
        y = y + D[:, None] * z
        y = jax.nn.gelu(jnp.swapaxes(y, 1, 2))
        g = y @ W_glu + b_glu
        g = g[..., :D_MODEL] * jax.nn.sigmoid(g[..., D_MODEL:])
        h = _layernorm(h + g, ln_gamma, ln_beta)
        out = h @ W_dec + b_dec
        out = jnp.swapaxes(out, 1, 2).reshape(Bsz, S, Hh, Ww)
        return out

    def _gn(v, G=32, eps=1e-05):
        B_, C_, H_, W_ = v.shape
        g = v.reshape(B_, G, C_ // G, H_, W_)
        m = jnp.mean(g, axis=(2, 3, 4), keepdims=True)
        s = jnp.var(g, axis=(2, 3, 4), keepdims=True)
        return ((g - m) / jnp.sqrt(s + eps)).reshape(v.shape)

    def _ln_c(v, eps=1e-06):
        m = jnp.mean(v, axis=1, keepdims=True)
        s = jnp.var(v, axis=1, keepdims=True)
        return (v - m) / jnp.sqrt(s + eps)

    def _ln_t(v, eps=1e-05):
        m = jnp.mean(v, axis=-1, keepdims=True)
        s = jnp.var(v, axis=-1, keepdims=True)
        return (v - m) / jnp.sqrt(s + eps)

    def _to_tokens(v):
        B_, C_, H_, W_ = v.shape
        return v.reshape(B_, C_, H_ * W_).transpose(0, 2, 1)

    def _from_tokens(t, like):
        B_, C_, H_, W_ = like.shape
        return t.transpose(0, 2, 1).reshape(B_, C_, H_, W_)
    x = x + _L0_conv_ref(_gn(x), L0_conv_b_rel_table, L0_conv_b_qkv_w, L0_conv_b_proj_w, L0_conv_b_proj_b, L0_conv_b_ln_g, L0_conv_b_ln_b, L0_conv_b_fc1_w, L0_conv_b_fc1_b, L0_conv_b_fc2_w, L0_conv_b_fc2_b, L0_conv_g_rel_table, L0_conv_g_qkv_w, L0_conv_g_proj_w, L0_conv_g_proj_b, L0_conv_g_ln_g, L0_conv_g_ln_b, L0_conv_g_fc1_w, L0_conv_g_fc1_b, L0_conv_g_fc2_w, L0_conv_g_fc2_b)
    x = x + _L1_conv_ref(_gn(x), L1_conv_W_enc, L1_conv_b_enc, L1_conv_log_dt, L1_conv_A_log_real, L1_conv_A_imag, L1_conv_C_real, L1_conv_C_imag, L1_conv_D, L1_conv_W_glu, L1_conv_b_glu, L1_conv_ln_gamma, L1_conv_ln_beta, L1_conv_W_dec, L1_conv_b_dec)
    return x

_drawn_inputs = setup_inputs


def setup_inputs(seed=0):
    import zlib

    import numpy as np

    out = dict(_drawn_inputs(seed))
    spreads = {'L0_conv_b_proj_b': (0.0, 0.465),
     'L0_conv_b_ln_g': (1.0, 0.2),
     'L0_conv_b_ln_b': (0.0, 0.8),
     'L0_conv_b_fc1_b': (0.0, 0.8),
     'L0_conv_b_fc2_b': (0.0, 0.8),
     'L0_conv_g_proj_b': (0.0, 0.1),
     'L0_conv_g_ln_g': (1.0, 0.2),
     'L0_conv_g_ln_b': (0.0, 0.1),
     'L0_conv_g_fc1_b': (0.0, 0.1),
     'L0_conv_g_fc2_b': (0.0, 0.1),
     'L1_conv_b_enc': (0.0, 0.1),
     'L1_conv_A_log_real': (-0.6931471824645996, 0.6),
     'L1_conv_b_glu': (0.0, 0.277),
     'L1_conv_ln_gamma': (1.0, 0.2),
     'L1_conv_ln_beta': (0.0, 0.1),
     'L1_conv_b_dec': (0.0, 0.1)}
    factors = {'L0_conv_b_rel_table': 8.0,
     'L0_conv_b_qkv_w': 4.818,
     'L0_conv_b_proj_w': 4.89,
     'L0_conv_g_rel_table': 31.017,
     'L0_conv_g_qkv_w': 4.036,
     'L0_conv_g_proj_w': 4.129}
    for name, (base, spread) in spreads.items():
        noise = np.random.default_rng([zlib.crc32(name.encode()), seed]).standard_normal(out[name].shape)
        drawn = base * np.exp(spread * noise) if base else spread * noise
        out[name] = jnp.asarray(drawn.astype(out[name].dtype))
    for name, factor in factors.items():
        out[name] = (out[name] * factor).astype(out[name].dtype)
    return out
```

```python
from contextlib import ExitStack

import numpy as np

import concourse.bass as bass
from concourse import mybir

ALU = mybir.AluOpType
ACT = mybir.ActivationFunctionType
AX = mybir.AxisListType
F32 = mybir.dt.float32
F16 = mybir.dt.float16

C = 32
IMG = 56
PX = IMG * IMG
HEADS, HD = 4, 8
E = 128
DM = 256
TAPS = 16
N2 = 4
CW = 448
NCH = PX // CW
TT = 112
TPC = CW // TT
ZC = C + 2
SIDE = {"b": 7, "g": 8}
PI = float(np.pi)


def columns(names):
    at, where = 0, {}
    for name, width in names:
        where[name] = (at, width)
        at += width
    return where, at


SHAPE_CONSTS = [("ident", 128), ("blockmean", 128), ("mean256", 128), ("center", 128), ("ident_rep", 96),
                ("qlo", 1), ("klo", 1), ("vmask", 64)]
STAGE = [("wq", 128), ("wk", 128), ("wv", 32), ("wp", 32), ("fc1", 128), ("fc2t", 96), ("fc1_b", 1),
         ("fc2_b", 1), ("proj_b", 1), ("ln_g", 1), ("ln_b", 1)]
S4D = [("wenc", 256), ("wenct", 64), ("wdec", 64), ("gamma", 2), ("beta", 2), ("benc", 2), ("bglu", 4), ("skip", 2),
       ("log_dt", 2), ("a_log_real", 8), ("a_imag", 8), ("c_real", 8), ("c_imag", 8), ("b_dec", 1)]
CONST_AT, CONST_W = columns(SHAPE_CONSTS)
STAGE_AT, STAGE_W = columns(STAGE)
S4D_AT, S4D_W = columns(S4D)


def vit_s4d_kernel(nc, x, x_win, consts, pick, stage_b, stage_g, s4d, w_glu, tab_b, tab_g, out):
    with ExitStack() as ctx:
        def sb(name, shape, dt=F32):
            return ctx.enter_context(nc.sbuf_tensor(name, shape, dt))

        def sem(name):
            return ctx.enter_context(nc.semaphore(name))

        ps = ctx.enter_context(nc.psum_tensor("ps", [128, 8, 512], F32))

        cst = sb("cst", [128, CONST_W])
        sel = sb("sel", [128, 128], F16)
        par = {"b": sb("par_b", [128, STAGE_W]), "g": sb("par_g", [128, STAGE_W])}
        p1 = sb("p1", [128, S4D_W])
        wglu = sb("wglu", [128, 2, 512])
        wglu_hi = sb("wglu_hi", [128, 2, 512], F16)
        wglu_lo = sb("wglu_lo", [128, 2, 512], F16)
        xr = sb("xr", [96, PX])
        ust = {k: sb("ust_" + k, [96, PX + 16], F16) for k in "bgs"}
        u32 = sb("u32", [96, PX])
        wst = {k: sb("wst_" + k, [96, 288], F16) for k in "bg"}
        wencst = sb("wencst", [96, 256], F16)
        bias32 = sb("bias32", [64, HEADS, 64])
        bt = {k: sb("bt_" + k, [128, HEADS, SIDE[k] ** 2], F16) for k in "bg"}
        q_hi = sb("q_hi", [128, 4, 448], F16)
        qs = sb("qs", [128, PX], F16)
        ks = sb("ks", [128, PX], F16)
        vm_buf = sb("vm_buf", [128, PX])
        vm = vm_buf[:, 0:2048].rearrange("p (b w a c) -> p b w a c", b=2, w=16, a=2)
        row_sum = sb("row_sum", [128, 2, 8 * HEADS])
        inv_sum = sb("inv_sum", [128, 2, 8 * HEADS])
        mx = sb("mx", [128, 2, HEADS * 8])
        pr = sb("pr", [128, 2, 8, HEADS, 64])
        pt = sb("pt", [128, 2, 8, 2, 128])
        on = sb("on", [32, 2, 448])
        sq = sb("sq", [128, 448])
        rc = sb("rc", [128, 448])
        veps = sb("veps", [TT, 16])
        rstd = sb("rstd", [TT, 16])
        rstd_wide = sb("rstd_wide", [TT, 4, 4, C])
        neghalf = sb("neghalf", [128, 32])
        yn = sb("yn", [128, 448])
        wpc = {k: sb("wpc_" + k, [32, 32]) for k in "bg"}
        pbc = {k: sb("pbc_" + k, [128, 1]) for k in "bg"}
        im = {k: sb("im_" + k, [128, 96]) for k in "bg"}
        aff = {k: sb("aff_" + k, [128, 96]) for k in "bg"}
        cvec = {k: sb("cvec_" + k, [96, 1]) for k in "bg"}
        center16 = sb("center16", [64, 32], F16)
        x1 = sb("x1", [96, PX])
        stats = sb("stats", [96, 2, NCH, 6])
        mv = sb("mv", [96, 2, 2])
        gr = sb("gr", [96, 2, 2])
        tk = sb("tk", [128, 40, 8])
        vre = sb("vre", [128, TAPS, 8])
        vim = sb("vim", [128, TAPS, 8])
        tmp = sb("tmp", [128, 4, 8, 8])
        arg = sb("arg", [128, 16])
        sc = sb("sc", [128, 16])
        taps = sb("taps", [128, 2, TAPS])
        ksum = sb("ksum", [128, TAPS, 4])
        cum = sb("cum", [128, 2, TAPS])
        edge = sb("edge", [128, 2, TAPS])
        ybias = sb("ybias", [128, 2])
        zero16 = sb("zero16", [128, TAPS])
        gt = sb("gt", [128, 2, TAPS * C])
        gw = sb("gw", [128, 4, 256])
        gw_hi = sb("gw_hi", [128, 4, 256], F16)
        gw_lo = sb("gw_lo", [128, 4, 256], F16)
        PAD = TAPS
        u4hi = sb("u4hi", [128, PAD + PX + 4], F16)
        u4lo = sb("u4lo", [128, PAD + PX + 4], F16)
        gy_hi = (qs, ks)
        ptv = pt[:, :, :, :, :].rearrange("p b c a q -> p b (c a q)")
        gy = [[ptv[:, b, 512 * a:512 * a + CW] for a in range(2)] for b in range(2)]
        sg = [ptv[:, 0, 1024 + 512 * a:1024 + 512 * a + CW] for a in range(2)]
        ag = [ptv[:, 1, 1024 + 512 * a:1024 + 512 * a + CW] for a in range(2)]
        prv = pr[:, :, :, :, :].rearrange("p b w h m -> p b (w h m)")
        rr = [[prv[:, b, 512 * a:512 * a + CW] for a in range(2)] for b in range(2)]
        rsq = [[prv[:, b, 1024 + 512 * a:1024 + 512 * a + CW] for a in range(2)] for b in range(2)]
        vmv = vm_buf[:, :].bitcast(F16)
        gy_lo = [vmv[:, a * PX:(a + 1) * PX] for a in range(2)]
        wdg = sb("wdg", [128, 2, 32])
        wdc = sb("wdc", [128, 2, C + 1])
        dcst = sb("dcst", [32, 1])
        msq = sb("msq", [112, 28])
        var1 = sb("var1", [112, 28])
        rs1 = sb("rs1", [112, 28])
        zt = sb("zt", [112, 28, 32])
        osb = u32[0:32, :]

        s_cst, s_pb, s_pg, s_p1, s_wg = (sem(n) for n in ("consts_in", "par_b_in", "par_g_in", "s4d_in", "wglu_in"))
        s_x = [sem(f"x_in{i}") for i in range(3)]
        s_tab = {k: sem("bias_in_" + k) for k in "bg"}
        s_btz = sem("bias_zeroed")
        s_bt = {k: sem("bias_split_" + k) for k in "bg"}
        s_prep = sem("weights_prepared_dve")
        s_ws = {k: sem("qkv_split_" + k) for k in "bg"}
        s_fold = {k: sem("fold_mm_" + k) for k in "bg"}
        s_folded = {k: sem("folded_" + k) for k in "bg"}
        s_gn = sem("group_norm_dve")
        s_uhi = {k: sem("u_hi_" + k) for k in "bgs"}
        s_ulo = {k: sem("u_lo_" + k) for k in "bgs"}
        s_qk = {k: sem("qk_mm_" + k) for k in "bg"}
        s_qkhi = {k: sem("qk_hi_" + k) for k in "bg"}
        s_qks = {k: sem("qk_split_" + k) for k in "bg"}
        s_v = {k: sem("v_mm_" + k) for k in "bg"}
        s_vm = {k: sem("v_masked_" + k) for k in "bg"}
        s_sc = {k: sem("scores_mm_" + k) for k in "bg"}
        s_mx = {k: sem("row_max_" + k) for k in "bg"}
        s_sub = {k: sem("max_subtracted_" + k) for k in "bg"}
        s_exp = {k: sem("exp_" + k) for k in "bg"}
        s_tr = {k: sem("transposed_mm_" + k) for k in "bg"}
        s_pt = {k: sem("transposed_out_" + k) for k in "bg"}
        s_pv = {k: sem("pv_mm_" + k) for k in "bg"}
        s_sum = {k: sem("row_sums_" + k) for k in "bg"}
        s_inv = {k: sem("row_inverse_" + k) for k in "bg"}
        s_nrm = {k: sem("normalised_" + k) for k in "bg"}
        s_wide = {k: sem("ln_rstd_wide_" + k) for k in "bg"}
        s_back = {k: sem("ln_rstd_back_mm_" + k) for k in "bg"}
        s_img = {k: sem("image_order_" + k) for k in "bg"}
        s_on = {k: sem("attention_out_" + k) for k in "bg"}
        s_pj = {k: sem("proj_mm_" + k) for k in "bg"}
        s_sq = {k: sem("ln_square_" + k) for k in "bg"}
        s_var = {k: sem("ln_var_mm_" + k) for k in "bg"}
        s_rs = {k: sem("ln_rstd_" + k) for k in "bg"}
        s_yn = {k: sem("ln_out_" + k) for k in "bg"}
        s_ff = {k: sem("ff_mm_" + k) for k in "bg"}
        s_x1 = sem("x1_ready")
        s_act = sem("tap_act")
        s_pool = sem("tap_pool")
        s_tapin = sem("tap_reciprocal")
        s_angles = sem("tap_angles")
        s_abs = sem("tap_abs")
        s_gnr = sem("group_norm_rstd")
        s_rsq = {k: sem("ln_power_" + k) for k in "bg"}
        s_rs1 = sem("s4d_ln_power")
        s_neg = sem("minus_half_ready")
        s_sel = sem("sel_in")
        s_xr = sem("x_image_in")
        s_ffo = sem("stage_b_out")
        s_prz = sem("pads_zeroed")
        s_u32 = sem("u_float32")
        s_taps = sem("taps_ready")
        s_gt = sem("tap_weights_t")
        s_gtm = sem("tap_weights_mm")
        s_gwc = sem("tap_weights_copied")
        s_gws = sem("tap_weights_split")
        s_wgs = sem("wglu_split")
        s_we = sem("wenc_split")
        s_edge = sem("edge_terms")
        s_wd = sem("dec_scaled")
        s_wdm = sem("dec_fold_mm")
        s_wdc = sem("dec_centered")
        s_padz = sem("pad_zeroed")
        s_sh = [sem(f"shifted_in{i}") for i in range(2)]
        s_cv = sem("conv_mm")
        s_cve = sem("conv_edge_added")
        s_g32 = sem("gelu_f32")
        s_ghi = sem("gelu_hi")
        s_glo = sem("gelu_lo")
        s_gg = sem("glu_gate_mm")
        s_ga = sem("glu_value_mm")
        s_gh = sem("enc_mm")
        s_sg = sem("sigmoid")
        s_ag = sem("gated")
        s_r = sem("residual_sum")
        s_rq = sem("residual_square")
        s_z = sem("dec_mm")
        s_m2 = sem("mean_square_copied")
        s_t1 = sem("token_stats")
        s_zt = sem("dec_scaled_rows")
        s_zb = sem("dec_back_mm")
        s_o = sem("out_ready")
        s_out = sem("out_stored")

        def const(name, rows=128):
            a, w = CONST_AT[name]
            return cst[0:rows, a:a + w]

        def weight(k, name, rows=128, first=0):
            a, w = STAGE_AT[name]
            return par[k][first:rows, a:a + w]

        def s4(name, rows=128):
            a, w = S4D_AT[name]
            return p1[0:rows, a:a + w]

        def geometry(k):
            s = SIDE[k]
            n = IMG // s
            return s, s * s, n, s * IMG

        def rows_of(k, g):
            n = IMG // SIDE[k]
            return [r for r in (2 * g, 2 * g + 1) if r < n]

        def tile_rows(k, t):
            n = IMG // SIDE[k]
            return [r for r in range(4 * t, 4 * t + 4) if r < n]

        def rows_done(k, g):
            return min(2 * g + 2, IMG // SIDE[k])

        def chunks_of(k):
            return (IMG // SIDE[k] + 1) // 2

        def ring_uses(k):
            uses = [("v", 0)]
            nch = chunks_of(k)
            for g in range(4):
                if g < 3:
                    uses.append(("v", g + 1))
                uses += [("t", nch * g + c) for c in range(nch)]
                if g == 2:
                    uses += [("n", 0)] + [("f", r) for r in tile_rows(k, 0)]
            uses += [("n", 1)] + [("f", r) for r in tile_rows(k, 1)]
            return uses

        ring = {k: {u: i for i, u in enumerate(ring_uses(k))} for k in "bg"}

        def ring_bank(k, use):
            return ps[:, 4 + ring[k][use] % 2, :]

        def ff_done_sem(k):
            return s_ffo if k == "b" else s_x1

        def wait_ring_free(eng, k, use):
            i = ring[k][use] - 2
            if i < 0:
                return
            kind, n = ring_uses(k)[i]
            eng.wait_ge({"v": s_vm[k], "t": s_pt[k], "n": s_yn[k], "f": ff_done_sem(k)}[kind], n + 1)

        block = ctx.enter_context(nc.Block())

        @block.sync
        def _(sp):
            for i in range(3):
                sp.dma_start(x1[32 * i:32 * i + 32, :], x_win).then_inc(s_x[i], 16)
            sp.dma_start(cst[:, :], consts).then_inc(s_cst, 16)
            for i in range(3):
                sp.dma_start(xr[32 * i:32 * i + 32, :], x).then_inc(s_xr, 16)
            for k, tab in (("b", tab_b), ("g", tab_g)):
                s, T, n, cw = geometry(k)
                if k == "g":
                    sp.wait_ge(s_bt["b"], 2)
                for y in range(s):
                    sp.dma_start(bias32[y * s:(y + 1) * s, :, 0:T],
                                 tab[:, :, (s - 1 - y) * s:(s - 1 - y) * s + T]).then_inc(s_tab[k], 16)
            sp.wait_ge(s_padz, 1)
            for half in range(2):
                lo, hi = (0, 4 * CW) if half == 0 else (4 * CW, PX)
                sp.wait_ge(s_ulo["s"], 4 if half == 0 else NCH)
                for s in range(4):
                    for dst, r0 in ((u4hi, 0), (u4lo, 32)):
                        sp.dma_start(dst[32 * s:32 * s + 32, PAD + s + lo:PAD + s + hi],
                                     ust["s"][r0:r0 + 32, lo:hi]).then_inc(s_sh[half], 16)
            for n in range(NCH):
                sp.wait_ge(s_o, n + 1)
                sp.dma_start(out[:, n * CW:(n + 1) * CW], osb[:, n * CW:(n + 1) * CW]).then_inc(s_out, 16)
            sp.wait_ge(s_out, 16 * NCH)

        @block.gpsimd
        def _(pool):
            steps = [0]

            def step(ins):
                steps[0] += 1
                ins.then_inc(s_pool, 1)
                pool.wait_ge(s_pool, steps[0])

            pool.dma_start(p1[:, :], s4d).then_inc(s_p1, 16)
            pool.dma_start(par["g"][:, :], stage_g).then_inc(s_pg, 16)
            pool.dma_start(wglu[:, :, :], w_glu).then_inc(s_wg, 16)
            nc.gpsimd.memset(bt["b"][:, :, :], 0.0)
            nc.gpsimd.memset(bt["g"][:, :, :], 0.0).then_inc(s_btz, 1)
            nc.gpsimd.memset(ust["b"][:, PX:PX + 16], 0.0)
            nc.gpsimd.memset(pr[:, :, :, :, :], 0.0).then_inc(s_prz, 1)
            nc.gpsimd.memset(u4hi[:, :], 0.0)
            nc.gpsimd.memset(u4lo[:, :], 0.0).then_inc(s_padz, 1)

            def term(i):
                return tk[:, i, :]

            def mul(o, a, b):
                step(nc.gpsimd.tensor_tensor(o, a, b, ALU.mult))

            def add(o, a, b, op=ALU.add):
                step(nc.gpsimd.tensor_tensor(o, a, b, op))

            def ts(o, a, s1, s2=None, op0=ALU.mult, op1=None):
                if s2 is None:
                    step(nc.gpsimd.tensor_scalar(o, a, s1, None, op0))
                else:
                    step(nc.gpsimd.tensor_scalar(o, a, s1, s2, op0, op1))

            def pair(a):
                return a.rearrange("p (a n) -> p a n", a=2)

            dt_b = tk[:, 0, 0:2].unsqueeze(2).broadcast_to([128, 2, N2])
            nc.gpsimd.memset(neghalf[:, :], -0.5).then_inc(s_neg, 1)
            pool.wait_ge(s_neg, 1)
            pool.wait_ge(s_gn, 3)
            nc.gpsimd.tensor_tensor(gr[:, 0, 0:1], mv[:, 0, 1:2], neghalf[0:96, 0:1], ALU.pow).then_inc(s_gnr, 1)
            pool.wait_ge(s_gnr, 1)
            pool.wait_ge(s_p1, 16)
            pool.wait_ge(s_act, 2)
            mul(pair(term(2)), pair(term(1)), dt_b)
            ts(term(2), term(2), -1.0)
            mul(pair(term(3)), pair(s4("a_imag")), dt_b)
            mul(term(19), term(1), term(1))
            mul(term(20), s4("a_imag"), s4("a_imag"))
            nc.gpsimd.tensor_tensor(term(19), term(19), term(20), ALU.add).then_inc(s_abs, 1)
            ts(term(4), term(2), 1.0 / 64, -0.5, ALU.mult, ALU.max)
            ts(term(5), term(4), 1.0 / 7, 1.0, ALU.mult, ALU.add)
            for j in range(6, 1, -1):
                mul(term(5), term(5), term(4))
                ts(term(5), term(5), 1.0 / j, 1.0, ALU.mult, ALU.add)
            mul(term(5), term(5), term(4))
            for _ in range(6):
                ts(term(6), term(5), 2.0, None, ALU.add)
                mul(term(5), term(5), term(6))
            ts(arg[:, 0:8], term(3), 0.5)
            ts(arg[:, 8:16], term(3), 0.5, PI / 2, ALU.mult, ALU.add)
            turns = tk[:, 8:10, :].rearrange("p a n -> p (a n)")
            part = tk[:, 10:12, :].rearrange("p a n -> p (a n)")
            MAGIC = float(3 << 22)
            ts(turns, arg[:, :], 1.0 / (2 * PI))
            ts(turns, turns, MAGIC, None, ALU.add)
            ts(turns, turns, MAGIC, None, ALU.subtract)
            ts(part, turns, 6.28125)
            add(arg[:, :], arg[:, :], part, ALU.subtract)
            ts(part, turns, 2 * PI - 6.28125)
            add(arg[:, :], arg[:, :], part, ALU.subtract)
            nc.gpsimd.tensor_scalar(arg[:, :], arg[:, :], 3.1415925, -3.1415925, ALU.min,
                                    ALU.max).then_inc(s_angles, 1)
            pool.wait_ge(s_act, 3)
            sh, ch = sc[:, 0:8], sc[:, 8:16]
            mul(term(13), sh, sh)
            ts(term(13), term(13), 2.0)
            mul(term(14), sh, ch)
            ts(term(14), term(14), 2.0)
            ts(term(15), term(13), -1.0, 1.0, ALU.mult, ALU.add)
            mul(term(16), term(5), term(15))
            add(term(16), term(16), term(13), ALU.subtract)
            ts(term(17), term(5), 1.0, None, ALU.add)
            mul(term(17), term(17), term(14))
            ts(term(18), term(16), 1.0, None, ALU.add)
            mul(term(22), term(17), s4("a_imag"))
            mul(term(23), term(16), term(1))
            add(term(22), term(22), term(23), ALU.subtract)
            mul(term(23), term(17), term(1))
            mul(term(24), term(16), s4("a_imag"))
            add(term(23), term(23), term(24))
            ts(term(23), term(23), -1.0)
            pool.wait_ge(s_tapin, 1)
            mul(term(22), term(22), term(21))
            mul(term(23), term(23), term(21))
            mul(term(24), term(22), s4("c_real"))
            mul(term(25), term(23), s4("c_imag"))
            add(term(24), term(24), term(25), ALU.subtract)
            mul(term(25), term(22), s4("c_imag"))
            mul(term(26), term(23), s4("c_real"))
            add(term(25), term(25), term(26))
            ts(vre[:, 0, :], term(24), 2.0)
            ts(vim[:, 0, :], term(25), 2.0)
            zr, zi = term(18), term(17)
            t, free = 1, 27
            while t < TAPS:
                def spread(a):
                    return a.unsqueeze(1).broadcast_to([128, t, 8])
                m = [tmp[:, i, 0:t, :] for i in range(4)]
                mul(m[0], vre[:, 0:t, :], spread(zr))
                mul(m[1], vim[:, 0:t, :], spread(zi))
                add(vre[:, t:2 * t, :], m[0], m[1], ALU.subtract)
                mul(m[2], vre[:, 0:t, :], spread(zi))
                mul(m[3], vim[:, 0:t, :], spread(zr))
                add(vim[:, t:2 * t, :], m[2], m[3])
                if 2 * t < TAPS:
                    nr, ni = term(free), term(free + 1)
                    mul(term(free + 2), zr, zr)
                    mul(term(free + 3), zi, zi)
                    add(nr, term(free + 2), term(free + 3), ALU.subtract)
                    mul(term(free + 2), zr, zi)
                    ts(ni, term(free + 2), 2.0)
                    zr, zi = nr, ni
                    free += 4
                t *= 2
            v4 = vre[:, :, :].rearrange("p t (a n) -> p t a n", a=2)
            k4 = ksum[:, :, :].rearrange("p t (a n) -> p t a n", a=2)
            add(k4, v4[:, :, :, 0:2], v4[:, :, :, 2:4])
            add(taps[:, :, :].rearrange("p a t -> p t a"), k4[:, :, :, 0], k4[:, :, :, 1])
            add(taps[:, :, 0:1], taps[:, :, 0:1], s4("skip").unsqueeze(2))
            for a in range(2):
                ins = nc.gpsimd.tensor_tensor(
                    gt[:, a, :].rearrange("p (t c) -> p t c", c=C),
                    s4("wenct")[:, a * C:(a + 1) * C].unsqueeze(1).broadcast_to([128, TAPS, C]),
                    taps[:, a, :].unsqueeze(2).broadcast_to([128, TAPS, C]), ALU.mult)
                ins.then_inc(s_gt, 1)
            nc.gpsimd.tensor_copy(wencst[:, :], s4("wenc", 96)).then_inc(s_we, 1)
            pool.wait_ge(s_we, 1)
            nc.gpsimd.tensor_tensor(wencst[64:96, :], p1[64:96, S4D_AT["wenc"][0]:S4D_AT["wenc"][0] + 256],
                                    wencst[64:96, :], ALU.subtract).then_inc(s_we, 1)
            pool.wait_ge(s_we, 2)
            pool.wait_ge(s_wg, 16)
            nc.gpsimd.tensor_copy(wglu_hi[:, :, :], wglu[:, :, :]).then_inc(s_wgs, 1)
            pool.wait_ge(s_wgs, 1)
            nc.gpsimd.tensor_tensor(wglu_lo[:, :, :], wglu[:, :, :], wglu_hi[:, :, :],
                                    ALU.subtract).then_inc(s_wgs, 1)
            for a in range(2):
                ins = nc.gpsimd.tensor_scalar(wdg[:, a, :], s4("wdec")[:, a * C:(a + 1) * C],
                                              s4("gamma")[:, a:a + 1], None, ALU.mult)
            ins.then_inc(s_wd, 1)
            def divide(k, g):
                s, T, n, cw = geometry(k)
                pool.wait_ge(s_inv[k], g + 1)
                v = pr[:, g % 2, 0:n, :, 0:T].rearrange("p w h m -> p (w h) m")
                nc.gpsimd.tensor_tensor(v, v, inv_sum[:, g % 2, 0:n * HEADS].unsqueeze(2)
                                        .broadcast_to([128, n * HEADS, T]), ALU.mult).then_inc(s_nrm[k], 1)
                pool.wait_ge(s_nrm[k], g + 1)

            def ln_power(k, t):
                tok = geometry(k)[3] // 4
                pool.wait_ge(s_rs[k], t + 1)
                if t == 1:
                    pool.wait_ge(s_back[k], 1)
                nc.gpsimd.tensor_tensor(rstd[0:tok, :], veps[0:tok, :], neghalf[0:tok, 0:16],
                                        ALU.pow).then_inc(s_rsq[k], 1)
                pool.wait_ge(s_rsq[k], t + 1)
                nc.gpsimd.tensor_copy(rstd_wide[0:tok, :, :, :].rearrange("p a q c -> p (a q) c"),
                                      rstd[0:tok, :].unsqueeze(2).broadcast_to([tok, 16, C])).then_inc(s_wide[k], 1)
                pool.wait_ge(s_wide[k], t + 1)

            def attention_steps(k):
                for g in range(4):
                    divide(k, g)
                    if g == 2:
                        ln_power(k, 0)
                ln_power(k, 1)

            attention_steps("b")
            for r in range(IMG // 8):
                pool.wait_ge(s_img["b"], 2)
                src = x1[:, r * CW:(r + 1) * CW].rearrange("p (y j x) -> p y j x", y=8, x=8)
                dst = ust["g"][:, r * CW:(r + 1) * CW].rearrange("p (j y x) -> p y j x", y=8, x=8)
                nc.gpsimd.tensor_copy(dst, src).then_inc(s_uhi["g"], 1)
                pool.wait_ge(s_uhi["g"], r + 1)
                nc.gpsimd.tensor_tensor(dst[32:64], src[32:64], dst[32:64], ALU.subtract).then_inc(s_ulo["g"], 1)
                pool.wait_ge(s_ulo["g"], r + 1)
            pool.wait_ge(s_gwc, 2)
            nc.gpsimd.tensor_copy(gw_hi[:, :, :], gw[:, :, :]).then_inc(s_gws, 1)
            pool.wait_ge(s_gws, 1)
            nc.gpsimd.tensor_tensor(gw_lo[:, :, :], gw[:, :, :], gw_hi[:, :, :], ALU.subtract).then_inc(s_gws, 1)
            attention_steps("g")
            pool.wait_ge(s_gn, 7)
            nc.gpsimd.tensor_tensor(gr[:, 1, 0:1], mv[:, 1, 1:2], neghalf[0:96, 0:1], ALU.pow).then_inc(s_gnr, 1)
            pool.wait_ge(s_gnr, 2)
            pool.wait_ge(s_t1, 4)
            nc.gpsimd.tensor_tensor(rs1[:, :], msq[:, :], neghalf[0:TT, 0:28], ALU.pow).then_inc(s_rs1, 1)

        @block.scalar
        def _(act):
            act.dma_start(par["b"][:, :], stage_b).then_inc(s_pb, 16)
            act.dma_start(sel[:, :], pick).then_inc(s_sel, 16)
            act.wait_ge(s_p1, 16)
            nc.scalar.activation(tk[:, 0, 0:2], s4("log_dt"), ACT.Exp).then_inc(s_act, 1)
            nc.scalar.activation(tk[:, 1, :], s4("a_log_real"), ACT.Exp).then_inc(s_act, 1)
            act.wait_ge(s_gn, 4)
            for i in range(3):
                act.wait_ge(s_x[i], 16)
            for n in range(4):
                c = slice(n * 784, (n + 1) * 784)
                nc.scalar.activation(ust["b"][:, c], x1[:, c], ACT.Identity, bias=gr[:, 0, 1:2],
                                     scale=gr[:, 0, 0:1]).then_inc(s_uhi["b"], 1)

            def qk_hi(k, i):
                cw = geometry(k)[3]
                act.wait_ge(s_qk[k], i + 1)
                if i >= 4:
                    act.wait_ge(s_qks[k], i - 3)
                nc.scalar.copy(q_hi[:, i % 4, 0:cw], ps[:, i % 4, 0:cw]).then_inc(s_qkhi[k], 1)

            def exp(k, g):
                s, T, n, cw = geometry(k)
                act.wait_ge(s_sub[k], g + 1)
                v = pr[:, g % 2, 0:n, :, 0:T].rearrange("p w h m -> p (w h) m")
                nc.scalar.activation(v, v, ACT.Exp).then_inc(s_exp[k], 1)

            def transposed_out(k, g):
                s, T, n, cw = geometry(k)
                nch = chunks_of(k)
                if g >= 2:
                    act.wait_ge(s_pv[k], rows_done(k, g - 2))
                elif k == "g":
                    act.wait_ge(s_pv["b"], 8)
                for c in range(nch):
                    i = nch * g + c
                    act.wait_ge(s_tr[k], i + 1)
                    cols = min(2, n - 2 * c)
                    nc.scalar.copy(pt[:, g % 2, 2 * c:2 * c + cols, :, :].rearrange("p c a q -> p (c a q)"),
                                   ring_bank(k, ("t", i))[:, 0:cols * 256]).then_inc(s_pt[k], 1)

            def attention_out(k, r):
                cw = geometry(k)[3]
                act.wait_ge(s_pv[k], r + 1)
                if r >= 2:
                    act.wait_ge(s_pj[k], r - 1)
                elif k == "g":
                    act.wait_ge(s_pj["b"], 8)
                nc.scalar.copy(on[:, r % 2, 0:cw], ps[0:32, 6, 0:cw]).then_inc(s_on[k], 1)

            def ln_square(k, t):
                cw = geometry(k)[3]
                nr = len(tile_rows(k, t))
                act.wait_ge(s_pj[k], 4 * t + nr)
                act.wait_ge(s_folded[k], 3)
                if t == 1:
                    act.wait_ge(s_var[k], 1)
                    act.wait_ge(s_yn[k], 1)
                nc.scalar.activation(rc[0:32 * nr, 0:cw], ps[0:32 * nr, 7, 0:cw], ACT.Identity,
                                     bias=pbc[k][0:32 * nr, :])
                nc.scalar.activation(sq[0:32 * nr, 0:cw], ps[0:32 * nr, 7, 0:cw], ACT.Square,
                                     bias=pbc[k][0:32 * nr, :]).then_inc(s_sq[k], 1)

            def block_out(t):
                cw = geometry("b")[3]
                for r in tile_rows("b", t):
                    act.wait_ge(s_ff["b"], r + 1)
                    if r == 0:
                        act.wait_ge(s_ulo["b"], 4)
                    nc.scalar.activation(u32[:, r * cw:(r + 1) * cw], ring_bank("b", ("f", r))[0:96, 0:cw],
                                         ACT.Identity, bias=cvec["b"][:, :]).then_inc(s_ffo, 1)

            for k in "bg":
                n = geometry(k)[2]
                for i in range(2 * n):
                    qk_hi(k, i)
                if k == "b":
                    act.wait_ge(s_angles, 1)
                    nc.scalar.activation(sc[:, :], arg[:, :], ACT.Sin).then_inc(s_act, 1)
                exp(k, 0)
                for g in range(4):
                    transposed_out(k, g)
                    if g < 3:
                        exp(k, g + 1)
                    for r in rows_of(k, g):
                        attention_out(k, r)
                    if g == 1:
                        ln_square(k, 0)
                    if g == 2 and k == "b":
                        block_out(0)
                ln_square(k, 1)
                if k == "b":
                    block_out(1)
                    for a in range(2):
                        act.wait_ge(s_gtm, a + 1)
                        nc.scalar.copy(gw[:, :, a * 128:(a + 1) * 128],
                                       ps[:, 2 + a, :].rearrange("p (j d) -> p j d", j=4)).then_inc(s_gwc, 1)
            act.wait_ge(s_gn, 8)
            for n in range(NCH):
                c = slice(n * CW, (n + 1) * CW)
                nc.scalar.activation(ust["s"][:, c], x1[:, c], ACT.Identity, bias=gr[:, 1, 1:2],
                                     scale=gr[:, 1, 0:1]).then_inc(s_uhi["s"], 1)
            act.wait_ge(s_edge, 3)
            for n in range(NCH):
                for a in range(2):
                    i = 2 * n + a
                    act.wait_ge(s_cv, i + 1)
                    if n == 0:
                        act.wait_ge(s_cve, a + 1)
                    if n >= 2:
                        act.wait_ge(s_glo, i - 3)
                    nc.scalar.activation(gy[n % 2][a], ps[:, i % 4, 0:CW], ACT.Gelu_apprx_tanh,
                                         bias=ybias[:, a:a + 1]).then_inc(s_g32, 1)
                    nc.scalar.activation(gy_hi[a][:, n * CW:(n + 1) * CW], ps[:, i % 4, 0:CW],
                                         ACT.Gelu_apprx_tanh, bias=ybias[:, a:a + 1]).then_inc(s_ghi, 1)
            for n in range(NCH):
                for a in range(2):
                    i = 2 * n + a
                    act.wait_ge(s_gg, i + 1)
                    if i >= 2:
                        act.wait_ge(s_ag, i - 1)
                    nc.scalar.activation(sg[a], ps[:, 3 * a, 0:CW], ACT.Sigmoid,
                                         bias=s4("bglu")[:, 2 + a:3 + a]).then_inc(s_sg, 1)
                for a in range(2):
                    act.wait_ge(s_r, 2 * n + a + 1)
                    if n >= 2:
                        act.wait_ge(s_z, TPC * (n - 1))
                    nc.scalar.activation(rsq[n % 2][a], rr[n % 2][a], ACT.Square).then_inc(s_rq, 1)

        @block.vector
        def _(dve):
            def group_norm(j, first):
                dve.wait_ge(s_gn, first)
                nc.vector.bn_aggr(mv[:, j, :], stats[:, j, :, :].rearrange("p n s -> p (n s)")).then_inc(s_gn, 1)
                dve.wait_ge(s_gn, first + 1)
                nc.vector.tensor_scalar(mv[:, j, 1:2], mv[:, j, 1:2], 1e-5, None, ALU.add).then_inc(s_gn, 1)
                dve.wait_ge(s_gnr, j + 1)
                nc.vector.tensor_scalar(gr[:, j, 1:2], mv[:, j, 0:1], gr[:, j, 0:1], -1.0, ALU.mult,
                                        ALU.mult).then_inc(s_gn, 1)
                dve.wait_ge(s_gn, first + 3)

            def split_weights(k):
                dve.wait_ge(s_pb if k == "b" else s_pg, 16)
                nc.vector.tensor_scalar(weight(k, "wq", 96), weight(k, "wq", 96), float(HD) ** 0.5, None,
                                        ALU.mult).then_inc(s_ws[k], 1)
                dve.wait_ge(s_ws[k], 1)
                nc.vector.tensor_copy(wst[k][:, :], par[k][0:96, 0:288]).then_inc(s_ws[k], 1)
                dve.wait_ge(s_ws[k], 2)
                nc.vector.tensor_tensor(wst[k][64:96, :], par[k][64:96, 0:288], wst[k][64:96, :],
                                        ALU.subtract).then_inc(s_ws[k], 1)

            def split_bias(k):
                T = geometry(k)[1]
                dve.wait_ge(s_tab[k], 16 * SIDE[k])
                dve.wait_ge(s_btz, 1)
                nc.vector.tensor_copy(bt[k][0:T, :, :], bias32[0:T, :, 0:T]).then_inc(s_bt[k], 1)
                dve.wait_ge(s_bt[k], 1)
                nc.vector.tensor_tensor(bt[k][64:64 + T, :, :], bias32[0:T, :, 0:T], bt[k][0:T, :, :],
                                        ALU.subtract).then_inc(s_bt[k], 1)

            def fold(k):
                dve.wait_ge(s_fold[k], 1)
                nc.vector.tensor_copy(wpc[k][:, :], ps[0:32, 7, 0:32])
                nc.vector.tensor_copy(pbc[k][:, :], ps[:, 7, 32:33])
                nc.vector.tensor_tensor(im[k][:, :], ps[:, 7, 64:160], const("ident_rep"),
                                        ALU.add).then_inc(s_folded[k], 1)
                dve.wait_ge(s_folded[k], 1)
                nc.vector.tensor_scalar(aff[k][:, :], im[k][:, :], weight(k, "ln_g"), None,
                                        ALU.mult).then_inc(s_folded[k], 1)
                dve.wait_ge(s_fold[k], 2)
                nc.vector.tensor_tensor(cvec[k][:, :], ps[0:96, 7, 256:257], weight(k, "fc2_b", 96),
                                        ALU.add).then_inc(s_folded[k], 1)

            def split_lo(k, c, n, src_scale):
                j, src = src_scale
                nc.vector.tensor_scalar(u32[32:64, c], src[32:64, c], gr[32:64, j, 0:1], gr[32:64, j, 1:2],
                                        ALU.mult, ALU.add).then_inc(s_u32, 1)
                dve.wait_ge(s_u32, n)
                dve.wait_ge(s_uhi[k], n if k == "b" else n - 4)
                nc.vector.tensor_tensor(ust[k][32:64, c], u32[32:64, c], ust[k][32:64, c],
                                        ALU.subtract).then_inc(s_ulo[k], 1)

            def qk_split(k, i):
                cw = geometry(k)[3]
                dve.wait_ge(s_qkhi[k], i + 1)
                dst, low = (qs, "qlo") if i % 2 == 0 else (ks, "klo")
                r = i // 2
                nc.vector.scalar_tensor_tensor(out=dst[:, r * cw:(r + 1) * cw], in0=q_hi[:, i % 4, 0:cw],
                                               scalar=const(low), in1=ps[:, i % 4, 0:cw], op0=ALU.mult,
                                               op1=ALU.add).then_inc(s_qks[k], 1)

            def v_mask(k, g):
                s, T, n, cw = geometry(k)
                dve.wait_ge(s_v[k], g + 1)
                if g >= 2:
                    dve.wait_ge(s_pv[k], rows_done(k, g - 2))
                elif k == "g":
                    dve.wait_ge(s_pv["b"], 8)
                nr = len(rows_of(k, g))
                src = ring_bank(k, ("v", g))[:, 0:nr * 256].rearrange("p (w c) -> p w c", c=C)
                mask = const("vmask").rearrange("p (a c) -> p a c", a=2)
                for a in range(2):
                    ins = nc.vector.tensor_tensor(vm[:, g % 2, 0:nr * 8, a, 0:32], src,
                                                  mask[:, a:a + 1, :].broadcast_to([128, nr * 8, C]), ALU.mult)
                ins.then_inc(s_vm[k], 1)

            def softmax_shift(k, g):
                s, T, n, cw = geometry(k)
                dve.wait_ge(s_sc[k], g + 1)
                v = ps[:, 0:4, 0:cw].rearrange("p h (w m) -> p h w m", m=T)
                m = mx[:, g % 2, 0:HEADS * n].rearrange("p (h w) -> p h w", h=HEADS)
                nc.vector.tensor_reduce(m, v, AX.X, ALU.max).then_inc(s_mx[k], 1)
                dve.wait_ge(s_mx[k], g + 1)
                if g >= 2:
                    dve.wait_ge(s_tr[k], chunks_of(k) * (g - 1))
                elif k == "g":
                    dve.wait_ge(s_tr["b"], 4 * chunks_of("b"))
                dve.wait_ge(s_prz, 1)
                nc.vector.tensor_tensor(pr[:, g % 2, 0:n, :, 0:T].rearrange("p w h m -> p h w m"), v,
                                        m.unsqueeze(3).broadcast_to([128, HEADS, n, T]),
                                        ALU.subtract).then_inc(s_sub[k], 1)

            def row_inverse(k, g):
                s, T, n, cw = geometry(k)
                dve.wait_ge(s_exp[k], g + 1)
                nc.vector.tensor_reduce(row_sum[:, g % 2, 0:n * HEADS],
                                        pr[:, g % 2, 0:n, :, 0:T].rearrange("p w h m -> p (w h) m"), AX.X,
                                        ALU.add).then_inc(s_sum[k], 1)
                dve.wait_ge(s_sum[k], g + 1)
                nc.vector.reciprocal(inv_sum[:, g % 2, 0:n * HEADS],
                                     row_sum[:, g % 2, 0:n * HEADS]).then_inc(s_inv[k], 1)

            def variance_eps(k, t):
                tok = geometry(k)[3] // 4
                dve.wait_ge(s_var[k], t + 1)
                nc.vector.tensor_scalar(veps[0:tok, :], ps[0:tok, 7, 448:464], 1e-5, None,
                                        ALU.add).then_inc(s_rs[k], 1)

            def layer_norm(k, t):
                cw = geometry(k)[3]
                np_ = 32 * len(tile_rows(k, t))
                dve.wait_ge(s_back[k], t + 1)
                if t == 1:
                    dve.wait_ge(s_ff[k], 4)
                nc.vector.tensor_tensor(yn[0:np_, 0:cw], ring_bank(k, ("n", t))[0:np_, 0:cw], rc[0:np_, 0:cw],
                                        ALU.mult).then_inc(s_yn[k], 1)

            def residual(t):
                cw = geometry("g")[3]
                for r in tile_rows("g", t):
                    c = slice(r * cw, (r + 1) * cw)
                    dve.wait_ge(s_ff["g"], r + 1)
                    dve.wait_ge(s_xr, 48)
                    nc.vector.scalar_tensor_tensor(out=u32[:, c], in0=ring_bank("g", ("f", r))[0:96, 0:cw],
                                                   scalar=cvec["g"][:, :], in1=xr[:, c], op0=ALU.add,
                                                   op1=ALU.add).then_inc(s_x1, 1)

            def to_image(k, t):
                cw = geometry(k)[3]
                done = tile_rows(k, t)[-1] + 1
                first = 4 * cw // C * t
                last = done * cw // C
                dve.wait_ge(s_ffo if k == "b" else s_x1, done)
                if t == 0 and k == "g":
                    dve.wait_ge(s_ulo["g"], IMG // 8)
                nc.vector.transpose(x1[:, :].rearrange("p (c k) -> p k c", c=C)[:, first:last, :],
                                    u32[:, first * C:last * C].rearrange("p (k c) -> p k c", c=C)
                                    ).then_inc(s_img[k], 1)

            split_weights("b")
            dve.wait_ge(s_cst, 16)
            nc.vector.tensor_copy(center16[0:32, :], const("center", 32)[:, 0:32])
            nc.vector.tensor_copy(center16[32:64, :], const("center", 32)[:, 0:32]).then_inc(s_prep, 1)
            for i in range(3):
                dve.wait_ge(s_x[i], 16)
            for n in range(NCH):
                ins = nc.vector.bn_stats(stats[:, 0, n, :], x1[:, n * CW:(n + 1) * CW])
            ins.then_inc(s_gn, 1)
            group_norm(0, 1)
            for n in range(4):
                split_lo("b", slice(n * 784, (n + 1) * 784), n + 1, (0, x1))
            fold("b")
            for k in "bg":
                n = geometry(k)[2]
                if k == "g":
                    fold("g")
                for i in range(2 * n):
                    qk_split(k, i)
                    if i == 7 and k == "b":
                        split_bias("b")
                        split_weights("g")
                        dve.wait_ge(s_abs, 1)
                        nc.vector.reciprocal(tk[:, 21, :], tk[:, 19, :]).then_inc(s_tapin, 1)
                v_mask(k, 0)
                softmax_shift(k, 0)
                row_inverse(k, 0)
                for g in range(4):
                    if g < 3:
                        v_mask(k, g + 1)
                        softmax_shift(k, g + 1)
                        if g == 2:
                            variance_eps(k, 0)
                        row_inverse(k, g + 1)
                    if g == 1 and k == "b":
                        split_bias("g")
                    if g == 2:
                        layer_norm(k, 0)
                        if k == "g":
                            residual(0)
                        to_image(k, 0)
                variance_eps(k, 1)
                layer_norm(k, 1)
                if k == "g":
                    residual(1)
                to_image(k, 1)
                if k == "b":
                    dve.wait_ge(s_gt, 2)
                    nc.vector.memset(zero16[:, :], 0.0).then_inc(s_edge, 1)
                    dve.wait_ge(s_edge, 1)
                    for a in range(2):
                        ins = nc.vector.tensor_tensor_scan(cum[:, a, :], taps[:, a, :], zero16[:, :], 0.0,
                                                           ALU.add, ALU.add)
                    ins.then_inc(s_edge, 1)
                    dve.wait_ge(s_edge, 2)
                    for a in range(2):
                        nc.vector.tensor_scalar(edge[:, a, :], cum[:, a, :], cum[:, a, TAPS - 1:TAPS],
                                                s4("benc")[:, a:a + 1], ALU.subtract, ALU.mult)
                        ins = nc.vector.tensor_tensor(ybias[:, a:a + 1], cum[:, a, TAPS - 1:TAPS],
                                                      s4("benc")[:, a:a + 1], ALU.mult)
                    ins.then_inc(s_edge, 1)
                    dve.wait_ge(s_wdm, 1)
                    for a in range(2):
                        nc.vector.tensor_tensor(wdc[:, a, 0:C], wdg[:, a, :], ps[:, 1, 0:C], ALU.subtract)
                        nc.vector.tensor_copy(wdc[:, a, C:C + 1], const("mean256")[:, 0:1])
                    nc.vector.tensor_tensor(dcst[:, :], ps[0:32, 1, 64:65], s4("b_dec", 32),
                                            ALU.add).then_inc(s_wdc, 1)
            dve.wait_ge(s_img["g"], 2)
            for n in range(NCH):
                ins = nc.vector.bn_stats(stats[:, 1, n, :], x1[:, n * CW:(n + 1) * CW])
            ins.then_inc(s_gn, 1)
            group_norm(1, 5)
            for n in range(NCH):
                split_lo("s", slice(n * CW, (n + 1) * CW), n + 5, (1, x1))
            for n in range(NCH):
                for a in range(2):
                    i = 2 * n + a
                    if n == 0:
                        dve.wait_ge(s_cv, i + 1)
                        dve.wait_ge(s_edge, 3)
                        nc.vector.tensor_tensor(ps[:, i % 4, 0:TAPS], ps[:, i % 4, 0:TAPS], edge[:, a, :],
                                                ALU.add).then_inc(s_cve, 1)
                for a in range(2):
                    i = 2 * n + a
                    dve.wait_ge(s_ghi, i + 1)
                    nc.vector.tensor_tensor(gy_lo[a][:, n * CW:(n + 1) * CW], gy[n % 2][a],
                                            gy_hi[a][:, n * CW:(n + 1) * CW], ALU.subtract).then_inc(s_glo, 1)
            for n in range(NCH):
                for a in range(2):
                    i = 2 * n + a
                    dve.wait_ge(s_ga, i + 1)
                    dve.wait_ge(s_sg, i + 1)
                    nc.vector.scalar_tensor_tensor(out=ag[a], in0=ps[:, 3 * a + 1, 0:CW],
                                                   scalar=s4("bglu")[:, a:a + 1], in1=sg[a], op0=ALU.add,
                                                   op1=ALU.mult).then_inc(s_ag, 1)
                    dve.wait_ge(s_ag, i + 1)
                    dve.wait_ge(s_gh, i + 1)
                    if n >= 2:
                        dve.wait_ge(s_z, TPC * (n - 1))
                    nc.vector.scalar_tensor_tensor(out=rr[n % 2][a], in0=ps[:, 3 * a + 2, 0:CW],
                                                   scalar=s4("benc")[:, a:a + 1], in1=ag[a], op0=ALU.add,
                                                   op1=ALU.add).then_inc(s_r, 1)
            dve.wait_ge(s_z, TPC * NCH)
            zv = ps[0:TT, 6:8, 0:14 * ZC].rearrange("p b (t c) -> p b t c", c=ZC)
            v2 = [a[:, :].rearrange("p (b t) -> p b t", b=2) for a in (msq, var1, rs1)]
            nc.vector.tensor_copy(v2[0], zv[:, :, :, C]).then_inc(s_t1, 1)
            dve.wait_ge(s_t1, 1)
            nc.vector.tensor_tensor(v2[1], v2[0], v2[0], ALU.mult).then_inc(s_t1, 1)
            dve.wait_ge(s_t1, 2)
            nc.vector.tensor_tensor(v2[2], zv[:, :, :, C + 1], v2[1], ALU.subtract).then_inc(s_t1, 1)
            dve.wait_ge(s_t1, 3)
            nc.vector.tensor_scalar(msq[:, :], rs1[:, :], 1e-5, None, ALU.add).then_inc(s_t1, 1)
            dve.wait_ge(s_rs1, 1)
            nc.vector.tensor_tensor(zt[:, :, :].rearrange("p (b t) c -> p b t c", b=2), zv[:, :, :, 0:C],
                                    v2[2].unsqueeze(3).broadcast_to([TT, 2, 14, C]),
                                    ALU.mult).then_inc(s_zt, 1)
            for n in range(NCH):
                c = slice(n * CW, (n + 1) * CW)
                dve.wait_ge(s_zb, n + 1)
                nc.vector.scalar_tensor_tensor(out=osb[:, c], in0=ps[0:32, n % 4, 0:CW], scalar=dcst[:, :],
                                               in1=x1[0:32, c], op0=ALU.add, op1=ALU.add).then_inc(s_o, 1)

        @block.tensor
        def _(pe):
            def fold(k):
                pe.wait_ge(s_cst, 16)
                pe.wait_ge(s_pb if k == "b" else s_pg, 16)
                bank = ps[:, 7, :]
                nc.tensor.matmul(bank[0:32, 0:32], weight(k, "wp", 32), const("center", 32)[:, 0:32],
                                 start=True, stop=True)
                nc.tensor.matmul(bank[:, 32:33], const("center", 32), weight(k, "proj_b", 32),
                                 start=True, stop=True)
                nc.tensor.matmul(bank[:, 64:160], weight(k, "fc1"), weight(k, "fc2t"), start=True,
                                 stop=True).then_inc(s_fold[k], 1)
                pe.wait_ge(s_folded[k], 1)
                nc.tensor.matmul(bank[0:96, 256:257], weight(k, "fc2t"), weight(k, "fc1_b"), start=True, stop=False)
                nc.tensor.matmul(bank[0:96, 256:257], im[k][0:32, :], weight(k, "ln_b", 32), start=False,
                                 stop=True).then_inc(s_fold[k], 1)

            def qk(k, i):
                cw = geometry(k)[3]
                r, a = i // 2, i % 2
                if i >= 4:
                    pe.wait_ge(s_qks[k], i - 3)
                elif k == "g":
                    pe.wait_ge(s_sub["b"], 4)
                if a == 0:
                    if k == "b":
                        pe.wait_ge(s_ulo["b"], min(4, ((r + 1) * cw + 783) // 784))
                    else:
                        pe.wait_ge(s_ulo["g"], r + 1)
                nc.tensor.matmul(ps[:, i % 4, 0:cw], wst[k][:, a * 128:(a + 1) * 128],
                                 ust[k][:, r * cw:(r + 1) * cw], start=True, stop=True).then_inc(s_qk[k], 1)

            def values(k, g):
                s, T, n, cw = geometry(k)
                wait_ring_free(pe, k, ("v", g))
                bank = ring_bank(k, ("v", g))
                for w2, r in enumerate(rows_of(k, g)):
                    for j in range(8):
                        jj = min(j, n - 1)
                        at = (r * n + jj) * T
                        for half in (0, 64):
                            ins = nc.tensor.matmul(bank[half:half + 64, (w2 * 8 + j) * C:(w2 * 8 + j + 1) * C],
                                                   ust[k][:, at:at + 64], wst[k][:, 256:288],
                                                   start=True, stop=True)
                ins.then_inc(s_v[k], 1)

            def scores(k, g):
                s, T, n, cw = geometry(k)
                if g == 0:
                    pe.wait_ge(s_sel, 16)
                    pe.wait_ge(s_qks[k], 2 * n)
                    pe.wait_ge(s_bt[k], 2)
                else:
                    pe.wait_ge(s_sub[k], g)
                both = len(rows_of(k, g)) == 2
                for first, rows in ([(0, 128)] if both else [(0, 64), (64, 64)]):
                    for h in range(HEADS):
                        nc.tensor.matmul(ps[first:first + rows, h, 0:cw].rearrange("p (w m) -> p w m", m=T),
                                         sel[:, 0:rows], bt[k][:, h:h + 1, :].broadcast_to([128, n, T]),
                                         start=True, stop=True)
                for w2, r in enumerate(rows_of(k, g)):
                    for j in range(n):
                        for h in range(HEADS):
                            hp = slice(32 * h, 32 * h + 32)
                            win = slice((r * n + j) * T, (r * n + j + 1) * T)
                            ins = nc.tensor.matmul(ps[64 * w2:64 * w2 + T, h, j * T:(j + 1) * T],
                                                   qs[hp, win], ks[hp, win],
                                                   start=False, stop=True, skip_group_check=True)
                ins.then_inc(s_sc[k], 1)

            def transposes(k, g):
                s, T, n, cw = geometry(k)
                pe.wait_ge(s_nrm[k], g + 1)
                for c in range(chunks_of(k)):
                    i = chunks_of(k) * g + c
                    wait_ring_free(pe, k, ("t", i))
                    bank = ring_bank(k, ("t", i))
                    for jj in range(min(2, n - 2 * c)):
                        j = 2 * c + jj
                        for a in range(2):
                            at = (jj * 2 + a) * 128
                            ins = nc.tensor.transpose(bank[:, at:at + 128],
                                                      pr[:, g % 2, j, 2 * a:2 * a + 2, :].rearrange("p h m -> p (h m)"),
                                                      const("ident"))
                    ins.then_inc(s_tr[k], 1)

            def attend(k, g):
                s, T, n, cw = geometry(k)
                pe.wait_ge(s_pt[k], chunks_of(k) * (g + 1))
                pe.wait_ge(s_vm[k], g + 1)
                for w2, r in enumerate(rows_of(k, g)):
                    if r >= 1:
                        pe.wait_ge(s_on[k], r)
                    for j in range(n):
                        for a in range(2):
                            ins = nc.tensor.matmul(
                                ps[0:32, 6, j * T:(j + 1) * T], vm[:, g % 2, w2 * 8 + j, a, :],
                                pt[:, g % 2, j, a, 64 * w2:64 * w2 + T],
                                start=(a == 0), stop=(a == 1))
                    ins.then_inc(s_pv[k], 1)
                    project(k, r)

            def project(k, r):
                cw = geometry(k)[3]
                q = r % 4
                if r == 4:
                    pe.wait_ge(s_rs[k], 1)
                if r == 0:
                    pe.wait_ge(s_folded[k], 3)
                    pe.wait_ge(s_prep, 1)
                pe.wait_ge(s_on[k], r + 1)
                o = ps[32 * q:32 * q + 32, 7, 0:cw]
                nc.tensor.matmul(o, wpc[k][:, :], on[:, r % 2, 0:cw], start=True, stop=False,
                                 skip_group_check=True)
                nc.tensor.matmul(o, center16[:, :], ust[k][0:64, r * cw:(r + 1) * cw], start=False,
                                 stop=True, skip_group_check=True).then_inc(s_pj[k], 1)

            def variance(k, t):
                tok = geometry(k)[3] // 4
                nr = len(tile_rows(k, t))
                pe.wait_ge(s_sq[k], t + 1)
                for a in range(4):
                    ins = nc.tensor.matmul(ps[0:tok, 7, 448 + 4 * a:452 + 4 * a],
                                           sq[0:32 * nr, a * tok:(a + 1) * tok],
                                           const("blockmean", 32 * nr)[:, 0:128:32], start=True, stop=True)
                ins.then_inc(s_var[k], 1)

            def spread_rstd(k, t):
                tok = geometry(k)[3] // 4
                pe.wait_ge(s_wide[k], t + 1)
                wait_ring_free(pe, k, ("n", t))
                for a in range(4):
                    ins = nc.tensor.transpose(ring_bank(k, ("n", t))[:, a * tok:(a + 1) * tok],
                                              rstd_wide[0:tok, a, :, :].rearrange("p q c -> p (q c)"),
                                              const("ident", TT)[0:tok, 0:tok])
                ins.then_inc(s_back[k], 1)

            def feed_forward(k, t):
                s, T, n, cw = geometry(k)
                pe.wait_ge(s_yn[k], t + 1)
                for q, r in enumerate(tile_rows(k, t)):
                    wait_ring_free(pe, k, ("f", r))
                    nc.tensor.matmul(ring_bank(k, ("f", r))[0:96, 0:cw], aff[k][32 * q:32 * q + 32, :],
                                     yn[32 * q:32 * q + 32, 0:cw].rearrange("p (j t) -> p t j", t=T),
                                     start=True, stop=True).then_inc(s_ff[k], 1)

            fold("b")
            for k in "bg":
                n = geometry(k)[2]
                pe.wait_ge(s_ws[k], 3)
                for i in range(2 * n):
                    qk(k, i)
                if k == "g":
                    pe.wait_ge(s_ffo, 8)
                values(k, 0)
                scores(k, 0)
                for g in range(4):
                    if g < 3:
                        values(k, g + 1)
                        scores(k, g + 1)
                    transposes(k, g)
                    if g == 2:
                        variance(k, 0)
                    attend(k, g)
                    if g == 2:
                        spread_rstd(k, 0)
                        feed_forward(k, 0)
                variance(k, 1)
                spread_rstd(k, 1)
                feed_forward(k, 1)
                if k == "b":
                    pe.wait_ge(s_gt, 2)
                    pe.wait_ge(s_sub["b"], 4)
                    for a in range(2):
                        for j in range(4):
                            ins = nc.tensor.transpose(ps[:, 2 + a, j * 128:(j + 1) * 128],
                                                      gt[:, a, j * 128:(j + 1) * 128], const("ident"))
                        ins.then_inc(s_gtm, 1)
                    pe.wait_ge(s_wd, 1)
                    for a in range(2):
                        nc.tensor.matmul(ps[:, 1, 0:C], const("mean256"), wdg[:, a, :], start=(a == 0),
                                         stop=(a == 1))
                    for a in range(2):
                        ins = nc.tensor.matmul(ps[0:32, 1, 64:65], s4("wdec")[:, a * C:(a + 1) * C],
                                               s4("beta")[:, a:a + 1], start=(a == 0), stop=(a == 1))
                    ins.then_inc(s_wdm, 1)
                    pe.wait_ge(s_gwc, 2)
                    pe.wait_ge(s_wdc, 1)
                    pe.wait_ge(s_rs["b"], 2)
                    fold("g")

            pe.wait_ge(s_gws, 2)
            for n in range(NCH):
                if n == 0:
                    pe.wait_ge(s_sh[0], 16 * 8)
                    pe.wait_ge(s_sub["g"], 4)
                if n == 4:
                    pe.wait_ge(s_sh[1], 16 * 8)
                for a in range(2):
                    i = 2 * n + a
                    if i >= 4:
                        pe.wait_ge(s_ghi, i - 3)
                    m = 0
                    for wt, ut in ((gw_hi, u4hi), (gw_hi, u4lo), (gw_lo, u4hi)):
                        for j in range(4):
                            at = PAD + n * CW - 4 * j
                            ins = nc.tensor.matmul(ps[:, i % 4, 0:CW], wt[:, j, a * 128:(a + 1) * 128],
                                                   ut[:, at:at + CW], start=(m == 0), stop=(m == 11))
                            m += 1
                    ins.then_inc(s_cv, 1)
            pe.wait_ge(s_wgs, 2)
            pe.wait_ge(s_we, 2)
            pe.wait_ge(s_ghi, 2 * NCH)
            pe.wait_ge(s_x1, NCH)
            pe.wait_ge(s_rs["g"], 2)
            pe.wait_ge(s_wdc, 1)

            def glu(n, half, a, bank, done):
                c = slice(n * CW, (n + 1) * CW)
                o = (half * 2 + a) * 128
                m = 0
                for wt, yt in ((wglu_hi, gy_hi), (wglu_hi, gy_lo), (wglu_lo, gy_hi)):
                    for b in range(2):
                        ins = nc.tensor.matmul(ps[:, bank, 0:CW], wt[:, b, o:o + 128], yt[b][:, c],
                                               start=(m == 0), stop=(m == 5))
                        m += 1
                ins.then_inc(done, 1)

            def decode(n):
                pe.wait_ge(s_r, 2 * n + 2)
                for q in range(TPC):
                    t = TPC * n + q
                    o = ps[0:TT, 6 + t // 14, (t % 14) * ZC:(t % 14) * ZC + ZC]
                    tok = slice(q * TT, (q + 1) * TT)
                    for a in range(2):
                        nc.tensor.matmul(o[:, 0:C + 1], rr[n % 2][a][:, tok], wdc[:, a, :], start=(a == 0),
                                         stop=(a == 1))
                    if q == 0:
                        pe.wait_ge(s_rq, 2 * n + 2)
                    for a in range(2):
                        ins = nc.tensor.matmul(o[:, C + 1:C + 2], rsq[n % 2][a][:, tok], const("mean256")[:, 0:1],
                                               start=(a == 0), stop=(a == 1))
                    ins.then_inc(s_z, 1)

            for n in range(NCH):
                pe.wait_ge(s_glo, 2 * n + 2)
                for a in range(2):
                    i = 2 * n + a
                    if n >= 1:
                        pe.wait_ge(s_sg, i - 1)
                    glu(n, 1, a, 3 * a, s_gg)
                    if n >= 1:
                        pe.wait_ge(s_ag, i - 1)
                    glu(n, 0, a, 3 * a + 1, s_ga)
                    if n >= 1:
                        pe.wait_ge(s_r, i - 1)
                    nc.tensor.matmul(ps[:, 3 * a + 2, 0:CW], wencst[:, a * 128:(a + 1) * 128],
                                     ust["s"][:, n * CW:(n + 1) * CW], start=True, stop=True).then_inc(s_gh, 1)
                if n >= 1:
                    decode(n - 1)
            decode(NCH - 1)
            pe.wait_ge(s_zt, 1)
            for n in range(NCH):
                if n >= 4:
                    pe.wait_ge(s_o, n - 3)
                for q in range(TPC):
                    ins = nc.tensor.transpose(ps[0:32, n % 4, q * TT:(q + 1) * TT], zt[:, TPC * n + q, :],
                                              const("ident", TT)[:, 0:TT])
                ins.then_inc(s_zb, 1)


def _stack(parts, rows=128):
    total = sum(a.shape[1] for a in parts)
    whole = np.zeros((rows, total), np.float32)
    at = 0
    for a in parts:
        whole[:a.shape[0], at:at + a.shape[1]] = a
        at += a.shape[1]
    return whole


def _shape_constants():
    ident = np.eye(128, dtype=np.float32)
    block = np.kron(np.eye(4), np.full((32, 32), 1 / 32)).astype(np.float32)
    center = np.tile((np.eye(32) - 1 / 32).astype(np.float32), (1, 4))
    rows = np.arange(128)
    low = [np.where(rows % 32 // HD == r, -1.0, 0.0).astype(np.float32)[:, None] for r in (2, 1)]
    head, column = rows // 64, np.arange(C) // HD
    mask = np.concatenate([(head[:, None] + 2 * a == column[None, :]) for a in range(2)], 1).astype(np.float32)
    return _stack([ident, block, np.full((128, 128), 1 / 256, np.float32), center,
                   np.tile(ident[:32, :32], (4, 3)), *low, mask])


def _pick():
    n = np.arange(128)
    return (n[:, None] % 64 == n[None, :] % 64).astype(np.float16)


def _stage(qkv_w, proj_w, proj_b, ln_g, ln_b, fc1_w, fc1_b, fc2_w, fc2_b):
    qkv = qkv_w.reshape(3, HEADS, HD, C)

    def spread(w):
        out = np.zeros((C, HEADS, 4, HD), np.float32)
        out[:, :, 0:3, :] = w.transpose(2, 0, 1)[:, :, None, :]
        return np.tile(out.reshape(C, 128), (3, 1))
    return _stack([spread(qkv[0]), spread(qkv[1]), np.tile(qkv[2].reshape(C, C).T, (3, 1)), proj_w,
                   np.tile(fc1_w, (1, 4)), np.tile(fc2_w.T, (1, 3)), fc1_b[:, None],
                   np.tile(fc2_b[:, None], (3, 1)), proj_b[:, None], np.tile(ln_g[:, None], (4, 1)),
                   ln_b[:, None]])


def _halves(a):
    a = a.reshape(2, 128, -1)
    return a.transpose(1, 0, 2).reshape(128, -1)


def _table(t, side):
    w = 2 * side - 1
    t = t[:w * w].reshape(w, w, HEADS)[::-1, ::-1].transpose(2, 0, 1)
    return np.stack([t[:, :, side - 1 - x:2 * side - 1 - x] for x in range(side)]).reshape(side, HEADS, w * side)


def kernel(x, **p):
    import concourse.bacc as _bacc
    from concourse.bass_utils import run_bass_kernel_spmd as _run

    p = {k: np.asarray(v) for k, v in p.items()}
    names = ("qkv_w", "proj_w", "proj_b", "ln_g", "ln_b", "fc1_w", "fc1_b", "fc2_w", "fc2_b")
    l1 = {k[len("L1_conv_"):]: v for k, v in p.items() if k.startswith("L1_conv_")}
    arrays = {
        "x": np.asarray(x).reshape(C, C, PX // C).transpose(1, 2, 0).reshape(C, PX),
        "x_win": np.asarray(x).reshape(C, 8, 7, 8, 7).transpose(0, 1, 3, 2, 4).reshape(C, PX),
        "consts": _shape_constants(),
        "pick": _pick(),
        "stage_b": _stage(*(p["L0_conv_b_" + n] for n in names)),
        "stage_g": _stage(*(p["L0_conv_g_" + n] for n in names)),
        "s4d": _stack([np.tile(l1["W_enc"], (3, 1)), _halves(l1["W_enc"].T), _halves(l1["W_dec"]),
                       *(_halves(l1[n]) for n in ("ln_gamma", "ln_beta", "b_enc")),
                       l1["b_glu"].reshape(4, 128).T,
                       *(_halves(l1[n]) for n in ("D", "log_dt", "A_log_real", "A_imag", "C_real", "C_imag")),
                       l1["b_dec"][:, None]]),
        "w_glu": _halves(l1["W_glu"]).reshape(128, 2, 2 * DM),
        "tab_b": _table(p["L0_conv_b_rel_table"], 7),
        "tab_g": _table(p["L0_conv_g_rel_table"], 8),
    }
    arrays = {k: np.ascontiguousarray(v) for k, v in arrays.items()}
    nc = _bacc.Bacc("TRN2", target_bir_lowering=False, num_devices=1)
    args = [nc.dram_tensor(k, v.shape, mybir.dt.from_np(v.dtype), kind="ExternalInput").ap()
            for k, v in arrays.items()]
    out = nc.dram_tensor("out", (C, PX), F32, kind="ExternalOutput").ap()
    vit_s4d_kernel(nc, *args, out)
    r = _run(nc, [arrays], core_ids=[0])
    return r.results[0]["out"].reshape(1, C, IMG, IMG)
```

```python
from contextlib import ExitStack

import numpy as np

import concourse.bass as bass
from concourse import mybir

ALU = mybir.AluOpType
ACT = mybir.ActivationFunctionType
AX = mybir.AxisListType
F32 = mybir.dt.float32
F16 = mybir.dt.float16

C = 32
IMG = 56
PX = IMG * IMG
HEADS, HD = 4, 8
E = 128
DM = 256
TAPS = 16
N2 = 4
CW = 448
NCH = PX // CW
TT = 112
TPC = CW // TT
ZH = C + 1
ZC = 2 * ZH + 1
SIDE = {"b": 7, "g": 8}
PI = float(np.pi)
SEGMENTS = ((0, 1), (1, 4), (4, 7))


def columns(names):
    at, where = 0, {}
    for name, width in names:
        where[name] = (at, width)
        at += width
    return where, at


SHAPE_CONSTS = [("ident", 128), ("blockmean", 128), ("mean256", 128), ("center", 128), ("ident_rep", 96),
                ("qlo", 1), ("klo", 1)]
STAGE = [("wq", 128), ("wk", 128), ("wv", 32), ("wp", 32), ("fc1", 128), ("fc2t", 96), ("fc1_b", 1),
         ("fc2_b", 1), ("proj_b", 1), ("ln_g", 1), ("ln_b", 1)]
S4D = [("wenc", 256), ("wenct", 64), ("wdec", 64), ("gamma", 2), ("beta", 2), ("benc", 2), ("bglu", 4), ("skip", 2),
       ("log_dt", 2), ("a_log_real", 8), ("a_imag", 8), ("c_real", 8), ("c_imag", 8), ("b_dec", 1)]
CONST_AT, CONST_W = columns(SHAPE_CONSTS)
STAGE_AT, STAGE_W = columns(STAGE)
S4D_AT, S4D_W = columns(S4D)


def vit_s4d_kernel(nc, x, x_win, consts, pick, stage_b, stage_g, s4d, w_glu, tab_b, tab_g, out):
    with ExitStack() as ctx:
        def sb(name, shape, dt=F32):
            return ctx.enter_context(nc.sbuf_tensor(name, shape, dt))

        def sem(name):
            return ctx.enter_context(nc.semaphore(name))

        ps = ctx.enter_context(nc.psum_tensor("ps", [128, 8, 512], F32))

        cst = sb("cst", [128, CONST_W])
        sel = sb("sel", [128, 128], F16)
        par = {"b": sb("par_b", [128, STAGE_W]), "g": sb("par_g", [128, STAGE_W])}
        p1 = sb("p1", [128, S4D_W])
        wglu = sb("wglu", [128, 2, 512])
        wglu_hi = sb("wglu_hi", [128, 2, 512], F16)
        wglu_lo = sb("wglu_lo", [128, 2, 512], F16)
        xr = sb("xr", [96, PX])
        ust = {k: sb("ust_" + k, [96, PX + 16], F16) for k in "bgs"}
        u32 = sb("u32", [96, PX])
        wst = {k: sb("wst_" + k, [96, 288], F16) for k in "bg"}
        wencst = sb("wencst", [96, 256], F16)
        bias32 = sb("bias32", [64, HEADS, 64])
        bt = {k: sb("bt_" + k, [128, HEADS, SIDE[k] ** 2], F16) for k in "bg"}
        q_hi = sb("q_hi", [128, 4, 448], F16)
        qs = sb("qs", [128, PX], F16)
        ks = sb("ks", [128, PX], F16)
        vm_buf = sb("vm_buf", [128, PX])
        vm = vm_buf[:, 0:2048].rearrange("p (b w a c) -> p b w a c", b=2, w=16, a=2)
        row_sum = sb("row_sum", [128, 2, 8 * HEADS])
        inv_sum = sb("inv_sum", [128, 2, 8 * HEADS])
        mx = sb("mx", [128, 2, HEADS * 8])
        pr = sb("pr", [128, 3, 8, HEADS, 64])
        pt = sb("pt", [128, 2, 8, 2, 128])
        on = sb("on", [64, 2, 448])
        sq = sb("sq", [128, 448])
        rc = sb("rc", [128, 448])
        veps = sb("veps", [TT, 8])
        rstd = sb("rstd", [TT, 8])
        rstd_wide = sb("rstd_wide", [TT, 4, 2, C])
        neghalf = sb("neghalf", [128, 32])
        yn = sb("yn", [128, 448])
        wpc = {k: sb("wpc_" + k, [64, 32]) for k in "bg"}
        pbc = {k: sb("pbc_" + k, [128, 1]) for k in "bg"}
        im = {k: sb("im_" + k, [128, 96]) for k in "bg"}
        aff = {k: sb("aff_" + k, [128, 96]) for k in "bg"}
        cvec = {k: sb("cvec_" + k, [96, 1]) for k in "bg"}
        center16 = sb("center16", [64, 32], F16)
        x1 = sb("x1", [96, PX])
        stats = sb("stats", [96, 2, NCH, 6])
        mv = sb("mv", [96, 2, 2])
        gr = sb("gr", [96, 2, 2])
        tk = sb("tk", [128, 40, 8])
        vre = sb("vre", [128, TAPS, 8])
        vim = sb("vim", [128, TAPS, 8])
        tmp = sb("tmp", [128, 4, 8, 8])
        arg = sb("arg", [128, 16])
        sc = sb("sc", [128, 16])
        taps = sb("taps", [128, 2, TAPS])
        ksum = sb("ksum", [128, TAPS, 4])
        cum = sb("cum", [128, 2, TAPS])
        edge = sb("edge", [128, 2, TAPS])
        ybias = sb("ybias", [128, 2])
        zero16 = sb("zero16", [128, TAPS])
        gt = sb("gt", [128, 2, TAPS * C])
        gw = sb("gw", [128, 4, 256])
        gw_hi = sb("gw_hi", [128, 4, 256], F16)
        gw_lo = sb("gw_lo", [128, 4, 256], F16)
        PAD = TAPS
        u4hi = sb("u4hi", [128, PAD + PX + 4], F16)
        u4lo = sb("u4lo", [128, PAD + PX + 4], F16)
        gy_hi = (qs, ks)
        ptv = pt[:, :, :, :, :].rearrange("p b c a q -> p b (c a q)")
        gy = [[ptv[:, b, 512 * a:512 * a + CW] for a in range(2)] for b in range(2)]
        sg = [ptv[:, 0, 1024 + 512 * a:1024 + 512 * a + CW] for a in range(2)]
        ag = [ptv[:, 1, 1024 + 512 * a:1024 + 512 * a + CW] for a in range(2)]
        prv = pr[:, :, :, :, :].rearrange("p b w h m -> p b (w h m)")
        rr = [[prv[:, b, 512 * a:512 * a + CW] for a in range(2)] for b in range(2)]
        prh = prv[:, 2, :].bitcast(F16)
        rr_hi = [[prh[:, 512 * (2 * b + a):512 * (2 * b + a) + CW] for a in range(2)] for b in range(2)]
        rr_lo = [[prh[:, 2048 + 512 * (2 * b + a):2048 + 512 * (2 * b + a) + CW] for a in range(2)] for b in range(2)]
        rsq = [[prv[:, b, 1024 + 512 * a:1024 + 512 * a + CW] for a in range(2)] for b in range(2)]
        vmv = vm_buf[:, :].bitcast(F16)
        gy_lo = [vmv[:, a * PX:(a + 1) * PX] for a in range(2)]
        wdg = sb("wdg", [128, 2, 32])
        wdc = sb("wdc", [128, 2, ZH])
        wdc_hl = sb("wdc_hl", [128, 2, 2 * ZH], F16)
        zs = sb("zs", [TT, 2, TPC, ZH])
        dcst = sb("dcst", [32, 1])
        var1 = sb("var1", [TT, 2, TPC])
        veps1 = sb("veps1", [TT, 2, TPC])
        rs1 = sb("rs1", [TT, 2, TPC])
        zt = sb("zt", [TT, 2, TPC, C])
        osb = u32[0:32, :]

        s_cst, s_pb, s_pg, s_p1, s_wg = (sem(n) for n in ("consts_in", "par_b_in", "par_g_in", "s4d_in", "wglu_in"))
        s_x = [sem(f"x_half{i}_in") for i in range(2)]
        s_tab = {k: sem("bias_in_" + k) for k in "bg"}
        s_btz = sem("bias_zeroed")
        s_bt = {k: sem("bias_split_" + k) for k in "bg"}
        s_prep = sem("weights_prepared_dve")
        s_ws = {k: sem("qkv_split_" + k) for k in "bg"}
        s_fold = {k: sem("fold_mm_" + k) for k in "bg"}
        s_folded = {k: sem("folded_" + k) for k in "bg"}
        s_gn = sem("group_norm_dve")
        s_uhi = {k: sem("u_hi_" + k) for k in "bgs"}
        s_ulo = {k: sem("u_lo_" + k) for k in "bgs"}
        s_ulop = {k: sem("u_lo_by_pool_" + k) for k in "bg"}
        s_qk = {k: sem("qk_mm_" + k) for k in "bg"}
        s_qkhi = {k: sem("qk_hi_" + k) for k in "bg"}
        s_qks = {k: sem("qk_split_" + k) for k in "bg"}
        s_v = {k: sem("v_mm_" + k) for k in "bg"}
        s_vm = {k: sem("v_out_" + k) for k in "bg"}
        s_sc = {k: sem("scores_mm_" + k) for k in "bg"}
        s_mx = {k: sem("row_max_" + k) for k in "bg"}
        s_sub = {k: sem("max_subtracted_" + k) for k in "bg"}
        s_exp = {k: sem("exp_" + k) for k in "bg"}
        s_tr = {k: sem("transposed_mm_" + k) for k in "bg"}
        s_pt = {k: sem("transposed_out_" + k) for k in "bg"}
        s_pv = {k: sem("pv_mm_" + k) for k in "bg"}
        s_sum = {k: sem("row_sums_" + k) for k in "bg"}
        s_inv = {k: sem("row_inverse_" + k) for k in "bg"}
        s_nrm = {k: sem("normalised_" + k) for k in "bg"}
        s_wide = {k: sem("ln_rstd_wide_" + k) for k in "bg"}
        s_back = {k: sem("ln_rstd_back_mm_" + k) for k in "bg"}
        s_img = {k: sem("image_order_" + k) for k in "bg"}
        s_on = {k: sem("attention_out_" + k) for k in "bg"}
        s_pj = {k: sem("proj_mm_" + k) for k in "bg"}
        s_sq = {k: sem("ln_square_" + k) for k in "bg"}
        s_var = {k: sem("ln_var_mm_" + k) for k in "bg"}
        s_rs = {k: sem("ln_rstd_" + k) for k in "bg"}
        s_yn = {k: sem("ln_out_" + k) for k in "bg"}
        s_ff = {k: sem("ff_mm_" + k) for k in "bg"}
        s_x1 = sem("x1_ready")
        s_act = sem("tap_act")
        s_pool = sem("tap_pool")
        s_tapin = sem("tap_reciprocal")
        s_angles = sem("tap_angles")
        s_abs = sem("tap_abs")
        s_gnr = sem("group_norm_rstd")
        s_rsq = {k: sem("ln_power_" + k) for k in "bg"}
        s_rs1 = sem("s4d_ln_power")
        s_neg = sem("minus_half_ready")
        s_sel = sem("sel_in")
        s_xr = sem("x_image_in")
        s_ffo = sem("stage_b_out")
        s_prz = sem("pads_zeroed")
        s_u32 = sem("u_float32")
        s_u32b = sem("u_float32_by_act")
        s_taps = sem("taps_ready")
        s_gt = sem("tap_weights_t")
        s_gtm = sem("tap_weights_mm")
        s_gwc = sem("tap_weights_copied")
        s_gws = sem("tap_weights_split")
        s_wgs = sem("wglu_split")
        s_we = sem("wenc_split")
        s_edge = sem("edge_terms")
        s_wd = sem("dec_scaled")
        s_wdm = sem("dec_fold_mm")
        s_wdc = sem("dec_centered")
        s_padz = sem("pad_zeroed")
        s_shhi = [sem(f"shifted_hi_in{i}") for i in range(len(SEGMENTS))]
        s_shlo = [sem(f"shifted_lo_in{i}") for i in range(len(SEGMENTS))]
        s_shpool = [sem(f"shifted_lo_by_pool_in{i}") for i in range(len(SEGMENTS))]
        s_first = sem("first_shifted_hi")
        s_cv = sem("conv_mm")
        s_cve = sem("conv_edge_added")
        s_g32 = sem("gelu_f32")
        s_ghi = sem("gelu_hi")
        s_glo = sem("gelu_lo")
        s_gg = sem("glu_gate_mm")
        s_ga = sem("glu_value_mm")
        s_gh = sem("enc_mm")
        s_sg = sem("sigmoid")
        s_ag = sem("gated")
        s_r = sem("residual_sum")
        s_rhi = sem("residual_hi")
        s_rlo = sem("residual_lo")
        s_rq = sem("residual_square")
        s_r2 = sem("residual_square_sum")
        s_z = sem("dec_mm")
        s_m2 = sem("mean_square_copied")
        s_t1 = sem("token_stats")
        s_zt = sem("dec_scaled_rows")
        s_zb = sem("dec_back_mm")
        s_o = sem("out_ready")
        s_out = sem("out_stored")

        def const(name, rows=128):
            a, w = CONST_AT[name]
            return cst[0:rows, a:a + w]

        def weight(k, name, rows=128, first=0):
            a, w = STAGE_AT[name]
            return par[k][first:rows, a:a + w]

        def s4(name, rows=128):
            a, w = S4D_AT[name]
            return p1[0:rows, a:a + w]

        def geometry(k):
            s = SIDE[k]
            n = IMG // s
            return s, s * s, n, s * IMG

        def rows_of(k, g):
            n = IMG // SIDE[k]
            return [r for r in (2 * g, 2 * g + 1) if r < n]

        def ln_rows(k, g):
            first = 64 * (g % 2)
            return slice(first, first + 32 * len(rows_of(k, g)))

        def chunks_of(k):
            return (IMG // SIDE[k] + 1) // 2

        def ring_uses(k):
            nch = chunks_of(k)
            uses = [("v", 0)] + [("t", c) for c in range(nch)] + [("v", 1)]
            for g in range(4):
                if g < 3:
                    uses += [("t", nch * (g + 1) + c) for c in range(nch)]
                if g < 2:
                    uses.append(("v", g + 2))
                if g >= 1:
                    uses += [("n", g - 1)] + [("f", r) for r in rows_of(k, g - 1)]
            uses += [("n", 3)] + [("f", r) for r in rows_of(k, 3)]
            return uses

        ring = {k: {u: i for i, u in enumerate(ring_uses(k))} for k in "bg"}

        def ring_bank(k, use):
            return ps[:, 4 + ring[k][use] % 2, :]

        def decoded(n):
            return ps[0:TT, 6 + n % 2, 0:TPC * ZC].rearrange("p (t c) -> p t c", c=ZC)

        GATE, VALUE, ENC = (4, 0), (5, 1), (2, 3)

        def back_bank(n):
            return 2 if n < NCH - 1 else 1

        def ff_done_sem(k):
            return s_ffo if k == "b" else s_x1

        def wait_ring_free(eng, k, use):
            i = ring[k][use] - 2
            if i < 0:
                return
            kind, n = ring_uses(k)[i]
            eng.wait_ge({"v": s_vm[k], "t": s_pt[k], "n": s_yn[k], "f": ff_done_sem(k)}[kind], n + 1)

        block = ctx.enter_context(nc.Block())

        @block.sync
        def _(sp):
            for half in range(2):
                c = slice(half * PX // 2, (half + 1) * PX // 2)
                for i in range(2):
                    sp.dma_start(x1[32 * i:32 * i + 32, c], x_win[:, c]).then_inc(s_x[half], 16)
            sp.dma_start(sel[:, :], pick).then_inc(s_sel, 16)
            for k, tab in (("b", tab_b), ("g", tab_g)):
                s, T, n, cw = geometry(k)
                if k == "g":
                    sp.wait_ge(s_bt["b"], 2)
                for y in range(s):
                    sp.dma_start(bias32[y * s:(y + 1) * s, :, 0:T],
                                 tab[:, :, (s - 1 - y) * s:(s - 1 - y) * s + T]).then_inc(s_tab[k], 16)
            for i in range(3):
                sp.dma_start(xr[32 * i:32 * i + 32, :], x).then_inc(s_xr, 16)
            sp.wait_ge(s_padz, 1)
            for seg, (first, last) in enumerate(SEGMENTS):
                sp.wait_ge(s_uhi["s"], last)
                for s in range(0 if seg else 2, 4):
                    sp.dma_start(u4hi[32 * s:32 * s + 32, PAD + s + first * CW:PAD + s + last * CW],
                                 ust["s"][0:32, first * CW:last * CW]).then_inc(s_shhi[seg], 16)
                sp.wait_ge(s_ulo["s"], last)
                for s in range(2, 4):
                    sp.dma_start(u4lo[32 * s:32 * s + 32, PAD + s + first * CW:PAD + s + last * CW],
                                 ust["s"][32:64, first * CW:last * CW]).then_inc(s_shlo[seg], 16)
            for n in range(NCH):
                sp.wait_ge(s_o, n + 1)
                sp.dma_start(out[:, n * CW:(n + 1) * CW], osb[:, n * CW:(n + 1) * CW]).then_inc(s_out, 16)
            sp.wait_ge(s_out, 16 * NCH)

        @block.gpsimd
        def _(pool):
            steps = [0]

            def step(ins):
                steps[0] += 1
                ins.then_inc(s_pool, 1)
                pool.wait_ge(s_pool, steps[0])

            pool.dma_start(p1[:, :], s4d).then_inc(s_p1, 16)
            pool.dma_start(par["g"][:, :], stage_g).then_inc(s_pg, 16)
            nc.gpsimd.memset(bt["b"][:, :, :], 0.0)
            nc.gpsimd.memset(bt["g"][:, :, :], 0.0).then_inc(s_btz, 1)
            nc.gpsimd.memset(neghalf[:, :], -0.5).then_inc(s_neg, 1)
            nc.gpsimd.memset(ust["b"][:, PX:PX + 16], 0.0)
            nc.gpsimd.memset(vm_buf[:, 0:2048], 0.0)
            nc.gpsimd.memset(pr[:, :, :, :, :], 0.0).then_inc(s_prz, 1)
            nc.gpsimd.memset(u4hi[:, 0:PAD + 4], 0.0)
            nc.gpsimd.memset(u4lo[:, 0:PAD + 4], 0.0).then_inc(s_padz, 1)
            pool.wait_ge(s_padz, 1)

            def term(i):
                return tk[:, i, :]

            def mul(o, a, b):
                step(nc.gpsimd.tensor_tensor(o, a, b, ALU.mult))

            def add(o, a, b, op=ALU.add):
                step(nc.gpsimd.tensor_tensor(o, a, b, op))

            def ts(o, a, s1, s2=None, op0=ALU.mult, op1=None):
                if s2 is None:
                    step(nc.gpsimd.tensor_scalar(o, a, s1, None, op0))
                else:
                    step(nc.gpsimd.tensor_scalar(o, a, s1, s2, op0, op1))

            def pair(a):
                return a.rearrange("p (a n) -> p a n", a=2)

            dt_b = tk[:, 0, 0:2].unsqueeze(2).broadcast_to([128, 2, N2])
            pool.wait_ge(s_gn, 3)
            nc.gpsimd.tensor_tensor(gr[:, 0, 0:1], mv[:, 0, 1:2], neghalf[0:96, 0:1], ALU.pow).then_inc(s_gnr, 1)
            pool.wait_ge(s_gnr, 1)
            pool.wait_ge(s_p1, 16)
            pool.wait_ge(s_act, 2)
            mul(pair(term(2)), pair(term(1)), dt_b)
            ts(term(2), term(2), -1.0)
            mul(pair(term(3)), pair(s4("a_imag")), dt_b)
            mul(term(19), term(1), term(1))
            mul(term(20), s4("a_imag"), s4("a_imag"))
            nc.gpsimd.tensor_tensor(term(19), term(19), term(20), ALU.add).then_inc(s_abs, 1)
            ts(term(4), term(2), 1.0 / 64, -0.5, ALU.mult, ALU.max)
            ts(term(5), term(4), 1.0 / 7, 1.0, ALU.mult, ALU.add)
            for j in range(6, 1, -1):
                mul(term(5), term(5), term(4))
                ts(term(5), term(5), 1.0 / j, 1.0, ALU.mult, ALU.add)
            mul(term(5), term(5), term(4))
            for _ in range(6):
                ts(term(6), term(5), 2.0, None, ALU.add)
                mul(term(5), term(5), term(6))
            ts(arg[:, 0:8], term(3), 0.5)
            ts(arg[:, 8:16], term(3), 0.5, PI / 2, ALU.mult, ALU.add)
            turns = tk[:, 8:10, :].rearrange("p a n -> p (a n)")
            part = tk[:, 10:12, :].rearrange("p a n -> p (a n)")
            MAGIC = float(3 << 22)
            ts(turns, arg[:, :], 1.0 / (2 * PI))
            ts(turns, turns, MAGIC, None, ALU.add)
            ts(turns, turns, MAGIC, None, ALU.subtract)
            ts(part, turns, 6.28125)
            add(arg[:, :], arg[:, :], part, ALU.subtract)
            ts(part, turns, 2 * PI - 6.28125)
            add(arg[:, :], arg[:, :], part, ALU.subtract)
            nc.gpsimd.tensor_scalar(arg[:, :], arg[:, :], 3.1415925, -3.1415925, ALU.min,
                                    ALU.max).then_inc(s_angles, 1)

            def tap_terms():
                pool.wait_ge(s_act, 3)
                sh, ch = sc[:, 0:8], sc[:, 8:16]
                mul(term(13), sh, sh)
                ts(term(13), term(13), 2.0)
                mul(term(14), sh, ch)
                ts(term(14), term(14), 2.0)
                ts(term(15), term(13), -1.0, 1.0, ALU.mult, ALU.add)
                mul(term(16), term(5), term(15))
                add(term(16), term(16), term(13), ALU.subtract)
                ts(term(17), term(5), 1.0, None, ALU.add)
                mul(term(17), term(17), term(14))
                ts(term(18), term(16), 1.0, None, ALU.add)
                mul(term(22), term(17), s4("a_imag"))
                mul(term(23), term(16), term(1))
                add(term(22), term(22), term(23), ALU.subtract)
                mul(term(23), term(17), term(1))
                mul(term(24), term(16), s4("a_imag"))
                add(term(23), term(23), term(24))
                ts(term(23), term(23), -1.0)
                pool.wait_ge(s_tapin, 1)
                mul(term(22), term(22), term(21))
                mul(term(23), term(23), term(21))
                mul(term(24), term(22), s4("c_real"))
                mul(term(25), term(23), s4("c_imag"))
                add(term(24), term(24), term(25), ALU.subtract)
                mul(term(25), term(22), s4("c_imag"))
                mul(term(26), term(23), s4("c_real"))
                add(term(25), term(25), term(26))
                ts(vre[:, 0, :], term(24), 2.0)
                ts(vim[:, 0, :], term(25), 2.0)

            z_power = [(term(18), term(17))] + [(term(27 + 4 * i), term(28 + 4 * i)) for i in range(3)]

            def tap_powers(levels):
                for level in levels:
                    t = 1 << level
                    zr, zi = z_power[level]

                    def spread(a):
                        return a.unsqueeze(1).broadcast_to([128, t, 8])
                    m = [tmp[:, i, 0:t, :] for i in range(4)]
                    mul(m[0], vre[:, 0:t, :], spread(zr))
                    mul(m[1], vim[:, 0:t, :], spread(zi))
                    add(vre[:, t:2 * t, :], m[0], m[1], ALU.subtract)
                    mul(m[2], vre[:, 0:t, :], spread(zi))
                    mul(m[3], vim[:, 0:t, :], spread(zr))
                    add(vim[:, t:2 * t, :], m[2], m[3])
                    if 2 * t < TAPS:
                        nr, ni = z_power[level + 1]
                        t2, t3 = term(29 + 4 * level), term(30 + 4 * level)
                        mul(t2, zr, zr)
                        mul(t3, zi, zi)
                        add(nr, t2, t3, ALU.subtract)
                        mul(t2, zr, zi)
                        ts(ni, t2, 2.0)

            def tap_weights():
                v4 = vre[:, :, :].rearrange("p t (a n) -> p t a n", a=2)
                k4 = ksum[:, :, :].rearrange("p t (a n) -> p t a n", a=2)
                add(k4, v4[:, :, :, 0:2], v4[:, :, :, 2:4])
                add(taps[:, :, :].rearrange("p a t -> p t a"), k4[:, :, :, 0], k4[:, :, :, 1])
                add(taps[:, :, 0:1], taps[:, :, 0:1], s4("skip").unsqueeze(2))
                for a in range(2):
                    ins = nc.gpsimd.tensor_tensor(
                        gt[:, a, :].rearrange("p (t c) -> p t c", c=C),
                        s4("wenct")[:, a * C:(a + 1) * C].unsqueeze(1).broadcast_to([128, TAPS, C]),
                        taps[:, a, :].unsqueeze(2).broadcast_to([128, TAPS, C]), ALU.mult)
                    ins.then_inc(s_gt, 1)
                nc.gpsimd.tensor_copy(wencst[:, :], s4("wenc", 96)).then_inc(s_we, 1)
                pool.wait_ge(s_we, 1)
                nc.gpsimd.tensor_tensor(wencst[64:96, :], p1[64:96, S4D_AT["wenc"][0]:S4D_AT["wenc"][0] + 256],
                                        wencst[64:96, :], ALU.subtract).then_inc(s_we, 1)
                pool.wait_ge(s_we, 2)

            def glu_weights():
                pool.wait_ge(s_wg, 16)
                nc.gpsimd.tensor_copy(wglu_hi[:, :, :], wglu[:, :, :]).then_inc(s_wgs, 1)
                pool.wait_ge(s_wgs, 1)
                nc.gpsimd.tensor_tensor(wglu_lo[:, :, :], wglu[:, :, :], wglu_hi[:, :, :],
                                        ALU.subtract).then_inc(s_wgs, 1)

            def dec_weights():
                for a in range(2):
                    ins = nc.gpsimd.tensor_scalar(wdg[:, a, :], s4("wdec")[:, a * C:(a + 1) * C],
                                                  s4("gamma")[:, a:a + 1], None, ALU.mult)
                ins.then_inc(s_wd, 1)

            pool.dma_start(wglu[:, :, :], w_glu).then_inc(s_wg, 16)

            def divide(k, g):
                s, T, n, cw = geometry(k)
                pool.wait_ge(s_inv[k], g + 1)
                v = pr[:, g % 3, 0:n, :, 0:T].rearrange("p w h m -> p (w h) m")
                nc.gpsimd.tensor_tensor(v, v, inv_sum[:, g % 2, 0:n * HEADS].unsqueeze(2)
                                        .broadcast_to([128, n * HEADS, T]), ALU.mult).then_inc(s_nrm[k], 1)
                pool.wait_ge(s_nrm[k], g + 1)

            def ln_power(k, g):
                tok, cols = geometry(k)[3] // 4, 4 * len(rows_of(k, g))
                pool.wait_ge(s_rs[k], g + 1)
                nc.gpsimd.tensor_tensor(rstd[0:tok, 0:cols], veps[0:tok, 0:cols], neghalf[0:tok, 0:cols],
                                        ALU.pow).then_inc(s_rsq[k], 1)
                pool.wait_ge(s_rsq[k], g + 1)

            def window_lo(n):
                c = slice(n * 784, (n + 1) * 784)
                pool.wait_ge(s_u32b, n)
                pool.wait_ge(s_uhi["b"], n + 1)
                nc.gpsimd.tensor_tensor(ust["b"][32:64, c], u32[32:64, c], ust["b"][32:64, c],
                                        ALU.subtract).then_inc(s_ulop["b"], 1)
                pool.wait_ge(s_ulop["b"], 1)

            def grid_lo(r):
                src = x1[32:64, r * CW:(r + 1) * CW].rearrange("p (y j x) -> p j y x", y=8, x=8)
                dst = ust["g"][32:64, r * CW:(r + 1) * CW].rearrange("p (j y x) -> p j y x", y=8, x=8)
                pool.wait_ge(s_uhi["g"], r + 1)
                nc.gpsimd.tensor_tensor(dst, src, dst, ALU.subtract).then_inc(s_ulop["g"], 1)
                pool.wait_ge(s_ulop["g"], r - 2)

            pool.wait_ge(s_angles, 1)
            window_lo(3)
            tap_terms()
            divide("b", 0)
            divide("b", 1)
            divide("b", 2)
            ln_power("b", 0)
            divide("b", 3)
            tap_powers((0,))
            ln_power("b", 1)
            tap_powers((1,))
            ln_power("b", 2)
            tap_powers((2,))
            ln_power("b", 3)
            for r in range(3, 7):
                grid_lo(r)
            tap_powers((3,))
            tap_weights()
            divide("g", 0)
            dec_weights()
            divide("g", 1)
            divide("g", 2)
            ln_power("g", 0)
            divide("g", 3)
            glu_weights()
            for g in range(1, 4):
                ln_power("g", g)
            pool.wait_ge(s_gn, 7)
            nc.gpsimd.tensor_tensor(gr[:, 1, 0:1], mv[:, 1, 1:2], neghalf[0:96, 0:1], ALU.pow).then_inc(s_gnr, 1)
            pool.wait_ge(s_gnr, 2)
            for seg, (first, last) in enumerate(SEGMENTS):
                pool.wait_ge(s_ulo["s"], last)
                for s in range(2):
                    pool.dma_start(u4lo[32 * s:32 * s + 32, PAD + s + first * CW:PAD + s + last * CW],
                                   ust["s"][32:64, first * CW:last * CW]).then_inc(s_shpool[seg], 16)
            def add_squares(n):
                pool.wait_ge(s_rq, 2 * n + 2)
                nc.gpsimd.tensor_tensor(rsq[n % 2][0], rsq[n % 2][0], rsq[n % 2][1], ALU.add).then_inc(s_r2, 1)
                pool.wait_ge(s_r2, n + 1)

            add_squares(0)
            for n in range(NCH):
                if n + 1 < NCH:
                    add_squares(n + 1)
                pool.wait_ge(s_t1, 4 * n + 4)
                nc.gpsimd.tensor_tensor(rs1[:, n % 2, :], veps1[:, n % 2, :], neghalf[0:TT, 0:TPC],
                                        ALU.pow).then_inc(s_rs1, 1)
                pool.wait_ge(s_rs1, n + 1)

        @block.scalar
        def _(act):
            act.dma_start(par["b"][:, :], stage_b).then_inc(s_pb, 16)
            act.dma_start(x1[64:96, 0:PX // 2], x_win[:, 0:PX // 2]).then_inc(s_x[0], 16)
            act.dma_start(x1[64:96, PX // 2:PX], x_win[:, PX // 2:PX]).then_inc(s_x[1], 16)
            act.dma_start(cst[:, :], consts).then_inc(s_cst, 16)
            act.wait_ge(s_p1, 16)
            nc.scalar.activation(tk[:, 0, 0:2], s4("log_dt"), ACT.Exp).then_inc(s_act, 1)
            nc.scalar.activation(tk[:, 1, :], s4("a_log_real"), ACT.Exp).then_inc(s_act, 1)
            act.wait_ge(s_gn, 4)

            def window_hi(n):
                c = slice(n * 784, (n + 1) * 784)
                nc.scalar.activation(ust["b"][:, c], x1[:, c], ACT.Identity, bias=gr[:, 0, 1:2],
                                     scale=gr[:, 0, 0:1]).then_inc(s_uhi["b"], 1)

            def window_f32(n):
                c = slice(n * 784, (n + 1) * 784)
                nc.scalar.activation(u32[32:64, c], x1[32:64, c], ACT.Identity, bias=gr[32:64, 0, 1:2],
                                     scale=gr[32:64, 0, 0:1]).then_inc(s_u32b, 1)

            def qk_hi(k, i):
                cw = geometry(k)[3]
                act.wait_ge(s_qk[k], i + 1)
                if i >= 4:
                    act.wait_ge(s_qks[k], i - 3)
                nc.scalar.copy(q_hi[:, i % 4, 0:cw], ps[:, 4 + i % 4, 0:cw]).then_inc(s_qkhi[k], 1)

            def value_out(k, g):
                n = geometry(k)[2]
                act.wait_ge(s_v[k], g + 1)
                if g >= 2:
                    act.wait_ge(s_pv[k], g - 1)
                elif k == "g":
                    act.wait_ge(s_pv["b"], 4)
                act.wait_ge(s_prz, 1)
                for w2 in range(len(rows_of(k, g))):
                    for p in range(2):
                        rows = slice(64 * p, 64 * p + 64)
                        src = ring_bank(k, ("v", g))[rows, w2 * 256:w2 * 256 + n * C]
                        src = src.rearrange("p (w a h d) -> p w a h d", a=2, h=2, d=HD)[:, :, :, p, :]
                        for a in range(2):
                            at = 16 * a + HD * p
                            ins = nc.scalar.copy(vm[rows, g % 2, w2 * 8:w2 * 8 + n, a, at:at + HD], src[:, :, a, :])
                ins.then_inc(s_vm[k], 1)

            def exp(k, g):
                s, T, n, cw = geometry(k)
                act.wait_ge(s_sub[k], 2 * g + 2)
                v = pr[:, g % 3, 0:n, :, 0:T].rearrange("p w h m -> p (w h) m")
                nc.scalar.activation(v, v, ACT.Exp).then_inc(s_exp[k], 1)

            def transposed_out(k, g):
                s, T, n, cw = geometry(k)
                nch = chunks_of(k)
                if g >= 2:
                    act.wait_ge(s_pv[k], g - 1)
                elif k == "g":
                    act.wait_ge(s_pv["b"], 4)
                for c in range(nch):
                    i = nch * g + c
                    act.wait_ge(s_tr[k], i + 1)
                    cols = min(2, n - 2 * c)
                    nc.scalar.copy(pt[:, g % 2, 2 * c:2 * c + cols, :, :].rearrange("p c a q -> p (c a q)"),
                                   ring_bank(k, ("t", i))[:, 0:cols * 256]).then_inc(s_pt[k], 1)

            def attention_out(k, g):
                cw = geometry(k)[3]
                np_ = 32 * len(rows_of(k, g))
                act.wait_ge(s_pv[k], g + 1)
                if g >= 2:
                    act.wait_ge(s_pj[k], 2 * g - 2)
                elif k == "g":
                    act.wait_ge(s_pj["b"], 8)
                nc.scalar.copy(on[0:np_, g % 2, 0:cw], ps[0:np_, 6, 0:cw]).then_inc(s_on[k], 1)

            def ln_square(k, g):
                cw = geometry(k)[3]
                rows = ln_rows(k, g)
                act.wait_ge(s_pj[k], rows_of(k, g)[-1] + 1)
                if g >= 2:
                    act.wait_ge(s_var[k], g - 1)
                    act.wait_ge(s_yn[k], g - 1)
                nc.scalar.activation(rc[rows, 0:cw], ps[rows, 7, 0:cw], ACT.Identity, bias=pbc[k][rows, :])
                nc.scalar.activation(sq[rows, 0:cw], ps[rows, 7, 0:cw], ACT.Square,
                                     bias=pbc[k][rows, :]).then_inc(s_sq[k], 1)

            def block_out(g):
                cw = geometry("b")[3]
                for r in rows_of("b", g):
                    act.wait_ge(s_ff["b"], r + 1)
                    if r == 0:
                        act.wait_ge(s_ulop["b"], 1)
                    nc.scalar.activation(u32[:, r * cw:(r + 1) * cw], ring_bank("b", ("f", r))[0:96, 0:cw],
                                         ACT.Identity, bias=cvec["b"][:, :]).then_inc(s_ffo, 1)

            def grid_hi(r):
                act.wait_ge(s_img["b"], 5)
                src = x1[:, r * CW:(r + 1) * CW].rearrange("p (y j x) -> p j y x", y=8, x=8)
                dst = ust["g"][:, r * CW:(r + 1) * CW].rearrange("p (j y x) -> p j y x", y=8, x=8)
                nc.scalar.copy(dst, src).then_inc(s_uhi["g"], 1)

            for k in "bg":
                n = geometry(k)[2]
                if k == "b":
                    window_hi(0)
                    window_hi(1)
                    window_f32(1)
                else:
                    for r in range(3):
                        grid_hi(r)
                for i in range(12):
                    if k == "b" and i in (4, 8):
                        window_hi(1 + i // 4)
                        window_f32(1 + i // 4)
                    if k == "b" and i == 8:
                        act.wait_ge(s_angles, 1)
                        nc.scalar.activation(sc[:, :], arg[:, :], ACT.Sin).then_inc(s_act, 1)
                    if k == "g" and i % 2 == 0 and 2 <= i <= 8:
                        grid_hi(2 + i // 2)
                    qk_hi(k, i)
                exp(k, 0)
                for i in range(12, 2 * n):
                    qk_hi(k, i)
                exp(k, 1)
                value_out(k, 0)
                transposed_out(k, 0)
                value_out(k, 1)
                exp(k, 2)
                for g in range(4):
                    if g < 3:
                        transposed_out(k, g + 1)
                    attention_out(k, g)
                    if g < 2:
                        value_out(k, g + 2)
                    ln_square(k, g)
                    if g == 0:
                        exp(k, 3)
                    if k == "b" and g >= 1:
                        block_out(g - 1)
                    if k == "g" and g == 1:
                        for a in range(2):
                            act.wait_ge(s_gtm, a + 1)
                            nc.scalar.copy(gw_hi[:, :, a * 128:(a + 1) * 128],
                                           ps[:, 2 + a, :].rearrange("p (j d) -> p j d", j=4)).then_inc(s_gwc, 1)
                if k == "b":
                    block_out(3)
            act.wait_ge(s_gn, 8)
            for n in range(NCH):
                c = slice(n * CW, (n + 1) * CW)
                nc.scalar.activation(ust["s"][:, c], x1[:, c], ACT.Identity, bias=gr[:, 1, 1:2],
                                     scale=gr[:, 1, 0:1]).then_inc(s_uhi["s"], 1)
                if n == 0:
                    act.wait_ge(s_padz, 1)
                    for s in range(2):
                        rows = slice(32 * s, 32 * s + 32)
                        ins = nc.scalar.activation(u4hi[rows, PAD + s:PAD + s + CW], x1[rows, 0:CW], ACT.Identity,
                                                   bias=gr[rows, 1, 1:2], scale=gr[rows, 1, 0:1])
                    ins.then_inc(s_first, 1)
            act.wait_ge(s_edge, 3)
            for n in range(NCH):
                for a in range(2):
                    i = 2 * n + a
                    act.wait_ge(s_cv, i + 1)
                    if n == 0:
                        act.wait_ge(s_cve, a + 1)
                    if n >= 2:
                        act.wait_ge(s_glo, i - 3)
                    nc.scalar.activation(gy[n % 2][a], ps[:, i % 4, 0:CW], ACT.Gelu_apprx_tanh,
                                         bias=ybias[:, a:a + 1]).then_inc(s_g32, 1)
                    nc.scalar.activation(gy_hi[a][:, n * CW:(n + 1) * CW], ps[:, i % 4, 0:CW],
                                         ACT.Gelu_apprx_tanh, bias=ybias[:, a:a + 1]).then_inc(s_ghi, 1)
            for n in range(NCH):
                for a in range(2):
                    i = 2 * n + a
                    act.wait_ge(s_gg, i + 1)
                    if i >= 2:
                        act.wait_ge(s_ag, i - 1)
                    nc.scalar.activation(sg[a], ps[:, GATE[a], 0:CW], ACT.Sigmoid,
                                         bias=s4("bglu")[:, 2 + a:3 + a]).then_inc(s_sg, 1)
                for a in range(2):
                    act.wait_ge(s_r, 2 * n + a + 1)
                    if n >= 2:
                        act.wait_ge(s_z, n - 1)
                    nc.scalar.copy(rr_hi[n % 2][a], rr[n % 2][a]).then_inc(s_rhi, 1)
                    nc.scalar.activation(rsq[n % 2][a], rr[n % 2][a], ACT.Square).then_inc(s_rq, 1)

        @block.vector
        def _(dve):
            def group_norm(j, first):
                dve.wait_ge(s_gn, first)
                nc.vector.bn_aggr(mv[:, j, :], stats[:, j, :, :].rearrange("p n s -> p (n s)")).then_inc(s_gn, 1)
                dve.wait_ge(s_gn, first + 1)
                nc.vector.tensor_scalar(mv[:, j, 1:2], mv[:, j, 1:2], 1e-5, None, ALU.add).then_inc(s_gn, 1)
                if j == 0:
                    fold("b")
                    fold_constant("b")
                dve.wait_ge(s_gnr, j + 1)
                nc.vector.tensor_scalar(gr[:, j, 1:2], mv[:, j, 0:1], gr[:, j, 0:1], -1.0, ALU.mult,
                                        ALU.mult).then_inc(s_gn, 1)
                dve.wait_ge(s_gn, first + 3)

            def split_weights(k):
                dve.wait_ge(s_pb if k == "b" else s_pg, 16)
                nc.vector.tensor_scalar(weight(k, "wq", 96), weight(k, "wq", 96), float(HD) ** 0.5, None,
                                        ALU.mult).then_inc(s_ws[k], 1)
                dve.wait_ge(s_ws[k], 1)
                nc.vector.tensor_copy(wst[k][:, :], par[k][0:96, 0:288]).then_inc(s_ws[k], 1)
                dve.wait_ge(s_ws[k], 2)
                nc.vector.tensor_tensor(wst[k][64:96, :], par[k][64:96, 0:288], wst[k][64:96, :],
                                        ALU.subtract).then_inc(s_ws[k], 1)

            def split_bias(k):
                T = geometry(k)[1]
                dve.wait_ge(s_tab[k], 16 * SIDE[k])
                dve.wait_ge(s_btz, 1)
                nc.vector.tensor_copy(bt[k][0:T, :, :], bias32[0:T, :, 0:T]).then_inc(s_bt[k], 1)
                dve.wait_ge(s_bt[k], 1)
                nc.vector.tensor_tensor(bt[k][64:64 + T, :, :], bias32[0:T, :, 0:T], bt[k][0:T, :, :],
                                        ALU.subtract).then_inc(s_bt[k], 1)

            def fold(k):
                dve.wait_ge(s_fold[k], 1)
                nc.vector.tensor_copy(wpc[k][0:32, :], ps[0:32, 3, 0:32])
                nc.vector.tensor_copy(wpc[k][32:64, :], ps[0:32, 3, 0:32])
                nc.vector.tensor_copy(pbc[k][:, :], ps[:, 3, 32:33])
                nc.vector.tensor_tensor(im[k][:, :], ps[:, 3, 64:160], const("ident_rep"),
                                        ALU.add).then_inc(s_folded[k], 1)
                dve.wait_ge(s_folded[k], 1)
                nc.vector.tensor_scalar(aff[k][:, :], im[k][:, :], weight(k, "ln_g"), None,
                                        ALU.mult).then_inc(s_folded[k], 1)

            def fold_constant(k):
                dve.wait_ge(s_fold[k], 2)
                nc.vector.tensor_tensor(cvec[k][:, :], ps[0:96, 3, 256:257], weight(k, "fc2_b", 96),
                                        ALU.add).then_inc(s_folded[k], 1)

            def split_lo(k, c, n):
                j = 0 if k == "b" else 1
                if k == "b" and n >= 1:
                    dve.wait_ge(s_u32b, n)
                else:
                    nc.vector.tensor_scalar(u32[32:64, c], x1[32:64, c], gr[32:64, j, 0:1], gr[32:64, j, 1:2],
                                            ALU.mult, ALU.add).then_inc(s_u32, 1)
                    dve.wait_ge(s_u32, 1 if k == "b" else n + 2)
                dve.wait_ge(s_uhi[k], n + 1)
                nc.vector.tensor_tensor(ust[k][32:64, c], u32[32:64, c], ust[k][32:64, c],
                                        ALU.subtract).then_inc(s_ulo[k], 1)

            def qk_split(k, i):
                cw = geometry(k)[3]
                dve.wait_ge(s_qkhi[k], i + 1)
                dst, low = (qs, "qlo") if i % 2 == 0 else (ks, "klo")
                r = i // 2
                nc.vector.scalar_tensor_tensor(out=dst[:, r * cw:(r + 1) * cw], in0=q_hi[:, i % 4, 0:cw],
                                               scalar=const(low), in1=ps[:, 4 + i % 4, 0:cw], op0=ALU.mult,
                                               op1=ALU.add).then_inc(s_qks[k], 1)

            def softmax_shift(k, g):
                s, T, n, cw = geometry(k)
                dve.wait_ge(s_sc[k], g + 1)
                v = ps[:, 0:4, 0:cw].rearrange("p h (w m) -> p h w m", m=T)
                m = mx[:, g % 2, 0:HEADS * n].rearrange("p (h w) -> p h w", h=HEADS)
                nc.vector.tensor_reduce(m, v, AX.X, ALU.max).then_inc(s_mx[k], 1)
                dve.wait_ge(s_mx[k], g + 1)
                if g >= 3:
                    dve.wait_ge(s_tr[k], chunks_of(k) * (g - 2))
                elif k == "g":
                    dve.wait_ge(s_tr["b"], 4 * chunks_of("b"))
                dve.wait_ge(s_prz, 1)
                for h in (slice(0, 2), slice(2, 4)):
                    nc.vector.tensor_tensor(pr[:, g % 3, 0:n, h, 0:T].rearrange("p w h m -> p h w m"), v[:, h, :, :],
                                            m[:, h, :].unsqueeze(3).broadcast_to([128, 2, n, T]),
                                            ALU.subtract).then_inc(s_sub[k], 1)

            def row_inverse(k, g):
                s, T, n, cw = geometry(k)
                dve.wait_ge(s_exp[k], g + 1)
                nc.vector.tensor_reduce(row_sum[:, g % 2, 0:n * HEADS],
                                        pr[:, g % 3, 0:n, :, 0:T].rearrange("p w h m -> p (w h) m"), AX.X,
                                        ALU.add).then_inc(s_sum[k], 1)
                dve.wait_ge(s_sum[k], g + 1)
                if g >= 2:
                    dve.wait_ge(s_nrm[k], g - 1)
                elif k == "g":
                    dve.wait_ge(s_nrm["b"], 4)
                nc.vector.reciprocal(inv_sum[:, g % 2, 0:n * HEADS],
                                     row_sum[:, g % 2, 0:n * HEADS]).then_inc(s_inv[k], 1)

            def variance_eps(k, g):
                tok, cols = geometry(k)[3] // 4, 4 * len(rows_of(k, g))
                dve.wait_ge(s_var[k], g + 1)
                nc.vector.tensor_scalar(veps[0:tok, 0:cols], ps[0:tok, 7, 448:448 + cols], 1e-5, None,
                                        ALU.add).then_inc(s_rs[k], 1)

            def spread_rows(k, g):
                tok, nr = geometry(k)[3] // 4, len(rows_of(k, g))
                dve.wait_ge(s_rsq[k], g + 1)
                if g >= 1:
                    dve.wait_ge(s_back[k], g)
                nc.vector.tensor_copy(rstd_wide[0:tok, :, 0:nr, :],
                                      rstd[0:tok, 0:4 * nr].rearrange("p (a q) -> p a q", a=4).unsqueeze(3)
                                      .broadcast_to([tok, 4, nr, C])).then_inc(s_wide[k], 1)

            def layer_norm(k, g):
                cw = geometry(k)[3]
                rows = ln_rows(k, g)
                dve.wait_ge(s_back[k], g + 1)
                if g >= 2:
                    dve.wait_ge(s_ff[k], 2 * g - 2)
                nc.vector.tensor_tensor(yn[rows, 0:cw], ring_bank(k, ("n", g))[0:rows.stop - rows.start, 0:cw], rc[rows, 0:cw],
                                        ALU.mult).then_inc(s_yn[k], 1)

            def residual(r):
                cw = geometry("g")[3]
                c = slice(r * cw, (r + 1) * cw)
                dve.wait_ge(s_ff["g"], r + 1)
                dve.wait_ge(s_xr, 48)
                nc.vector.scalar_tensor_tensor(out=u32[:, c], in0=ring_bank("g", ("f", r))[0:96, 0:cw],
                                               scalar=cvec["g"][:, :], in1=xr[:, c], op0=ALU.add,
                                               op1=ALU.add).then_inc(s_x1, 1)

            def to_image(k, first, last):
                nc.vector.transpose(x1[:, :].rearrange("p (c k) -> p k c", c=C)[:, first:last, :],
                                    u32[:, first * C:last * C].rearrange("p (k c) -> p k c", c=C)
                                    ).then_inc(s_img[k], 1)

            def block_to_image(first, last):
                cw = geometry("b")[3]
                dve.wait_ge(s_ffo, last)
                to_image("b", first * cw // C, last * cw // C)

            def row_to_image(r):
                residual(r)
                image_row(r)

            def image_row(r):
                dve.wait_ge(s_x1, r + 1)
                if r == 0:
                    dve.wait_ge(s_ulop["g"], 4)
                to_image("g", 14 * r, 14 * (r + 1))
                dve.wait_ge(s_img["g"], r + 1)
                ins = nc.vector.bn_stats(stats[:, 1, r, :], x1[:, :].rearrange("p (c k) -> p c k", c=C)
                                         [:, :, 14 * r:14 * (r + 1)])
                if r == NCH - 1:
                    ins.then_inc(s_gn, 1)

            def grid_lo(r):
                src = x1[32:64, r * CW:(r + 1) * CW].rearrange("p (y j x) -> p j y x", y=8, x=8)
                dst = ust["g"][32:64, r * CW:(r + 1) * CW].rearrange("p (j y x) -> p j y x", y=8, x=8)
                dve.wait_ge(s_uhi["g"], r + 1)
                nc.vector.tensor_tensor(dst, src, dst, ALU.subtract).then_inc(s_ulo["g"], 1)

            def window_lo(n):
                split_lo("b", slice(n * 784, (n + 1) * 784), n)

            def tap_sums():
                dve.wait_ge(s_gt, 2)
                nc.vector.memset(zero16[:, :], 0.0).then_inc(s_edge, 1)
                dve.wait_ge(s_edge, 1)
                for a in range(2):
                    ins = nc.vector.tensor_tensor_scan(cum[:, a, :], taps[:, a, :], zero16[:, :], 0.0,
                                                       ALU.add, ALU.add)
                ins.then_inc(s_edge, 1)
                dve.wait_ge(s_edge, 2)
                for a in range(2):
                    nc.vector.tensor_scalar(edge[:, a, :], cum[:, a, :], cum[:, a, TAPS - 1:TAPS],
                                            s4("benc")[:, a:a + 1], ALU.subtract, ALU.mult)
                    ins = nc.vector.tensor_tensor(ybias[:, a:a + 1], cum[:, a, TAPS - 1:TAPS],
                                                  s4("benc")[:, a:a + 1], ALU.mult)
                ins.then_inc(s_edge, 1)

            def s4d_weights():
                for a in range(2):
                    dve.wait_ge(s_gwc, a + 1)
                    nc.vector.tensor_tensor(gw_lo[:, :, a * 128:(a + 1) * 128],
                                            ps[:, 2 + a, :].rearrange("p (j d) -> p j d", j=4),
                                            gw_hi[:, :, a * 128:(a + 1) * 128], ALU.subtract).then_inc(s_gws, 1)
                dve.wait_ge(s_wdm, 1)
                for a in range(2):
                    nc.vector.tensor_tensor(wdc[:, a, 0:C], wdg[:, a, :], ps[:, 1, 0:C], ALU.subtract)
                    nc.vector.tensor_copy(wdc[:, a, C:C + 1], const("mean256")[:, 0:1])
                nc.vector.tensor_tensor(dcst[:, :], ps[0:32, 1, 64:65], s4("b_dec", 32),
                                        ALU.add).then_inc(s_wdc, 1)
                dve.wait_ge(s_wdc, 1)
                nc.vector.tensor_copy(wdc_hl[:, :, 0:ZH], wdc[:, :, :]).then_inc(s_wdc, 1)
                dve.wait_ge(s_wdc, 2)
                nc.vector.tensor_tensor(wdc_hl[:, :, ZH:2 * ZH], wdc[:, :, :], wdc_hl[:, :, 0:ZH],
                                        ALU.subtract).then_inc(s_wdc, 1)

            split_weights("b")
            for n in range(NCH):
                dve.wait_ge(s_x[(n + 1) * CW > PX // 2], 48)
                ins = nc.vector.bn_stats(stats[:, 0, n, :], x1[:, n * CW:(n + 1) * CW])
            ins.then_inc(s_gn, 1)
            dve.wait_ge(s_cst, 16)
            nc.vector.tensor_copy(center16[0:32, :], const("center", 32)[:, 0:32])
            nc.vector.tensor_copy(center16[32:64, :], const("center", 32)[:, 0:32]).then_inc(s_prep, 1)
            group_norm(0, 1)
            for k in "bg":
                n = geometry(k)[2]
                if k == "b":
                    window_lo(0)
                    split_bias("b")
                    window_lo(1)
                    for i in range(8):
                        qk_split("b", i)
                    dve.wait_ge(s_abs, 1)
                    nc.vector.reciprocal(tk[:, 21, :], tk[:, 19, :]).then_inc(s_tapin, 1)
                    window_lo(2)
                else:
                    for r in range(3):
                        grid_lo(r)
                    for r in range(4):
                        qk_split("g", 2 * r)
                        qk_split("g", 2 * r + 1)
                softmax_shift(k, 0)
                for i in range(8, 12):
                    qk_split(k, i)
                softmax_shift(k, 1)
                row_inverse(k, 0)
                for i in range(12, 2 * n):
                    qk_split(k, i)
                softmax_shift(k, 2)
                row_inverse(k, 1)
                row_inverse(k, 2)
                softmax_shift(k, 3)
                variance_eps(k, 0)
                row_inverse(k, 3)
                for g in range(3):
                    if g:
                        variance_eps(k, g)
                    if k == "g" and g == 1:
                        tap_sums()
                    if k == "g" and g == 2:
                        s4d_weights()
                    spread_rows(k, g)
                    layer_norm(k, g)
                    if k == "b":
                        if g == 0:
                            split_bias("g")
                            split_weights("g")
                        if g == 1:
                            fold("g")
                        if g < 2:
                            block_to_image(2 * g, 2 * g + 2)
                    elif g < 2:
                        for r in rows_of("g", g):
                            row_to_image(r)
                variance_eps(k, 3)
                if k == "g":
                    row_to_image(4)
                spread_rows(k, 3)
                if k == "g":
                    residual(5)
                layer_norm(k, 3)
                if k == "g":
                    image_row(5)
                    row_to_image(6)
                else:
                    block_to_image(4, 6)
                    fold_constant("g")
                    block_to_image(6, 7)
                    block_to_image(7, 8)
            group_norm(1, 5)
            for n in range(NCH):
                split_lo("s", slice(n * CW, (n + 1) * CW), n)
            for n in range(NCH):
                for a in range(2):
                    i = 2 * n + a
                    if n == 0:
                        dve.wait_ge(s_cv, i + 1)
                        dve.wait_ge(s_edge, 3)
                        nc.vector.tensor_tensor(ps[:, i % 4, 0:TAPS], ps[:, i % 4, 0:TAPS], edge[:, a, :],
                                                ALU.add).then_inc(s_cve, 1)
                for a in range(2):
                    i = 2 * n + a
                    dve.wait_ge(s_ghi, i + 1)
                    nc.vector.tensor_tensor(gy_lo[a][:, n * CW:(n + 1) * CW], gy[n % 2][a],
                                            gy_hi[a][:, n * CW:(n + 1) * CW], ALU.subtract).then_inc(s_glo, 1)
            def token_stats(n):
                z = decoded(n)
                v, e = (a[:, n % 2, :] for a in (var1, veps1))
                m = zs[:, n % 2, :, C]
                dve.wait_ge(s_z, n + 1)
                nc.vector.tensor_copy(zs[:, n % 2, :, :], z[:, :, 0:ZH]).then_inc(s_t1, 1)
                dve.wait_ge(s_t1, 4 * n + 1)
                nc.vector.tensor_tensor(zs[:, n % 2, :, :], z[:, :, ZH:2 * ZH], zs[:, n % 2, :, :],
                                        ALU.add).then_inc(s_t1, 1)
                dve.wait_ge(s_t1, 4 * n + 2)
                nc.vector.tensor_tensor(v, m, m, ALU.mult).then_inc(s_t1, 1)
                dve.wait_ge(s_t1, 4 * n + 3)
                nc.vector.scalar_tensor_tensor(out=e, in0=z[:, :, 2 * ZH], scalar=1e-5, in1=v, op0=ALU.add,
                                               op1=ALU.subtract).then_inc(s_t1, 1)

            def token_scale(n):
                dve.wait_ge(s_rs1, n + 1)
                if n >= 2:
                    dve.wait_ge(s_zb, n - 1)
                nc.vector.tensor_tensor(zt[:, n % 2, :, :], zs[:, n % 2, :, 0:C],
                                        rs1[:, n % 2, :].unsqueeze(2).broadcast_to([TT, TPC, C]),
                                        ALU.mult).then_inc(s_zt, 1)

            def output(n):
                c = slice(n * CW, (n + 1) * CW)
                dve.wait_ge(s_zb, n + 1)
                nc.vector.scalar_tensor_tensor(out=osb[:, c], in0=ps[0:32, back_bank(n), 0:CW], scalar=dcst[:, :],
                                               in1=x1[0:32, c], op0=ALU.add, op1=ALU.add).then_inc(s_o, 1)

            for n in range(NCH):
                for a in range(2):
                    i = 2 * n + a
                    dve.wait_ge(s_ga, i + 1)
                    dve.wait_ge(s_sg, i + 1)
                    nc.vector.scalar_tensor_tensor(out=ag[a], in0=ps[:, VALUE[a], 0:CW],
                                                   scalar=s4("bglu")[:, a:a + 1], in1=sg[a], op0=ALU.add,
                                                   op1=ALU.mult).then_inc(s_ag, 1)
                    dve.wait_ge(s_ag, i + 1)
                    dve.wait_ge(s_gh, i + 1)
                    if n >= 2:
                        dve.wait_ge(s_z, n - 1)
                    nc.vector.scalar_tensor_tensor(out=rr[n % 2][a], in0=ps[:, ENC[a], 0:CW],
                                                   scalar=s4("benc")[:, a:a + 1], in1=ag[a], op0=ALU.add,
                                                   op1=ALU.add).then_inc(s_r, 1)
                for a in range(2):
                    dve.wait_ge(s_rhi, 2 * n + a + 1)
                    nc.vector.tensor_tensor(rr_lo[n % 2][a], rr[n % 2][a], rr_hi[n % 2][a],
                                            ALU.subtract).then_inc(s_rlo, 1)
                if n >= 1:
                    token_stats(n - 1)
                if n >= 2:
                    output(n - 2)
                if n >= 1:
                    token_scale(n - 1)
            token_stats(NCH - 1)
            output(NCH - 2)
            token_scale(NCH - 1)
            output(NCH - 1)

        @block.tensor
        def _(pe):
            def fold(k):
                pe.wait_ge(s_cst, 16)
                pe.wait_ge(s_pb if k == "b" else s_pg, 16)
                bank = ps[:, 3, :]
                nc.tensor.matmul(bank[0:32, 0:32], weight(k, "wp", 32), const("center", 32)[:, 0:32],
                                 start=True, stop=True)
                nc.tensor.matmul(bank[:, 32:33], const("center", 32), weight(k, "proj_b", 32),
                                 start=True, stop=True)
                nc.tensor.matmul(bank[:, 64:160], weight(k, "fc1"), weight(k, "fc2t"), start=True,
                                 stop=True).then_inc(s_fold[k], 1)

            def fold_constant(k):
                pe.wait_ge(s_folded[k], 1)
                bank = ps[:, 3, :]
                nc.tensor.matmul(bank[0:96, 256:257], weight(k, "fc2t"), weight(k, "fc1_b"), start=True, stop=False)
                nc.tensor.matmul(bank[0:96, 256:257], im[k][0:32, :], weight(k, "ln_b", 32), start=False,
                                 stop=True).then_inc(s_fold[k], 1)

            def qk(k, i):
                cw = geometry(k)[3]
                r, a = i // 2, i % 2
                if i >= 4:
                    pe.wait_ge(s_qks[k], i - 3)
                elif i == 0 and k == "g":
                    pe.wait_ge(s_ffo, 8)
                elif i == 3 and k == "g":
                    pe.wait_ge(s_rs["b"], 4)
                if a == 0:
                    if k == "b":
                        pe.wait_ge(*(s_ulo["b"], r // 2 + 1) if r < 6 else (s_ulop["b"], 1))
                    else:
                        pe.wait_ge(*(s_ulo["g"], r + 1) if r < 3 else (s_ulop["g"], r - 2))
                nc.tensor.matmul(ps[:, 4 + i % 4, 0:cw], wst[k][:, a * 128:(a + 1) * 128],
                                 ust[k][:, r * cw:(r + 1) * cw], start=True, stop=True).then_inc(s_qk[k], 1)

            def values(k, g):
                s, T, n, cw = geometry(k)
                wait_ring_free(pe, k, ("v", g))
                if g == 0:
                    pe.wait_ge(s_qks[k], 2 * n)
                bank = ring_bank(k, ("v", g))
                for w2, r in enumerate(rows_of(k, g)):
                    for j in range(n):
                        at = (r * n + j) * T
                        for half in (0, 64):
                            ins = nc.tensor.matmul(bank[half:half + 64, (w2 * 8 + j) * C:(w2 * 8 + j + 1) * C],
                                                   ust[k][:, at:at + 64], wst[k][:, 256:288],
                                                   start=True, stop=True)
                ins.then_inc(s_v[k], 1)

            def bias(k, g):
                s, T, n, cw = geometry(k)
                if g == 0:
                    pe.wait_ge(s_folded[k], 3)
                    pe.wait_ge(s_sel, 16)
                    pe.wait_ge(s_bt[k], 2)
                both = len(rows_of(k, g)) == 2
                for h in range(HEADS):
                    if (g > 0 or k == "g") and h % 2 == 0:
                        pe.wait_ge(s_sub[k if g else "b"], 2 * (g or 4) - 1 + h // 2)
                    for first, rows in ([(0, 128)] if both else [(0, 64), (64, 64)]):
                        nc.tensor.matmul(ps[first:first + rows, h, 0:cw].rearrange("p (w m) -> p w m", m=T),
                                         sel[:, 0:rows], bt[k][:, h:h + 1, :].broadcast_to([128, n, T]),
                                         start=True, stop=True)

            def scores(k, g):
                s, T, n, cw = geometry(k)
                if g:
                    bias(k, g)
                pe.wait_ge(s_qks[k], min(4 * g + 4, 2 * n))
                for j in range(n):
                    for i in range(HEADS):
                        for w2, r in enumerate(rows_of(k, g)):
                            h = (i + 2 * w2) % HEADS
                            hp = slice(32 * h, 32 * h + 32)
                            win = slice((r * n + j) * T, (r * n + j + 1) * T)
                            ins = nc.tensor.matmul(ps[64 * w2:64 * w2 + T, h, j * T:(j + 1) * T],
                                                   qs[hp, win], ks[hp, win],
                                                   start=False, stop=True, skip_group_check=True)
                ins.then_inc(s_sc[k], 1)

            def transpose_pair(k, g, c):
                n = geometry(k)[2]
                i = chunks_of(k) * g + c
                if c == 0:
                    pe.wait_ge(s_nrm[k], g + 1)
                wait_ring_free(pe, k, ("t", i))
                bank = ring_bank(k, ("t", i))
                for jj in range(min(2, n - 2 * c)):
                    j = 2 * c + jj
                    for a in range(2):
                        at = (jj * 2 + a) * 128
                        ins = nc.tensor.transpose(bank[:, at:at + 128],
                                                  pr[:, g % 3, j, 2 * a:2 * a + 2, :].rearrange("p h m -> p (h m)"),
                                                  const("ident"))
                ins.then_inc(s_tr[k], 1)

            def attend_pair(k, g, c):
                s, T, n, cw = geometry(k)
                if c == 0:
                    pe.wait_ge(s_pt[k], chunks_of(k) * (g + 1))
                    pe.wait_ge(s_vm[k], g + 1)
                    if g >= 1:
                        pe.wait_ge(s_on[k], g)
                    elif k == "g":
                        pe.wait_ge(s_on["b"], 4)
                for j in range(2 * c, min(2 * c + 2, n)):
                    for a in range(2):
                        for w2 in range(len(rows_of(k, g))):
                            ins = nc.tensor.matmul(
                                ps[32 * w2:32 * w2 + 32, 6, j * T:(j + 1) * T], vm[:, g % 2, w2 * 8 + j, a, :],
                                pt[:, g % 2, j, a, 64 * w2:64 * w2 + T],
                                start=(a == 0), stop=(a == 1))
                if c == chunks_of(k) - 1:
                    ins.then_inc(s_pv[k], 1)

            def project(k, r):
                cw = geometry(k)[3]
                q = r % 4
                if r in (2, 4, 6):
                    pe.wait_ge(s_rs[k], r // 2)
                if r == 0:
                    pe.wait_ge(s_prep, 1)
                pe.wait_ge(s_on[k], r // 2 + 1)
                o = ps[32 * q:32 * q + 32, 7, 0:cw]
                half = slice(32 * (r % 2), 32 * (r % 2) + 32)
                nc.tensor.matmul(o, wpc[k][half, :], on[half, r // 2 % 2, 0:cw], start=True, stop=False,
                                 skip_group_check=True)
                nc.tensor.matmul(o, center16[:, :], ust[k][0:64, r * cw:(r + 1) * cw], start=False,
                                 stop=True, skip_group_check=True).then_inc(s_pj[k], 1)

            def variance(k, g):
                tok = geometry(k)[3] // 4
                rows, nr = ln_rows(k, g), len(rows_of(k, g))
                pe.wait_ge(s_sq[k], g + 1)
                for a in range(4):
                    ins = nc.tensor.matmul(ps[0:tok, 7, 448 + nr * a:448 + nr * (a + 1)],
                                           sq[rows, a * tok:(a + 1) * tok],
                                           const("blockmean")[rows, rows.start:rows.stop:32], start=True, stop=True)
                ins.then_inc(s_var[k], 1)

            def spread_rstd(k, g):
                tok = geometry(k)[3] // 4
                nr = len(rows_of(k, g))
                pe.wait_ge(s_wide[k], g + 1)
                wait_ring_free(pe, k, ("n", g))
                for a in range(4):
                    ins = nc.tensor.transpose(ring_bank(k, ("n", g))[0:32 * nr, a * tok:(a + 1) * tok],
                                              rstd_wide[0:tok, a, 0:nr, :].rearrange("p q c -> p (q c)"),
                                              const("ident", TT)[0:tok, 0:tok])
                ins.then_inc(s_back[k], 1)

            def feed_forward(k, r):
                s, T, n, cw = geometry(k)
                pe.wait_ge(s_yn[k], r // 2 + 1)
                q = r % 4
                wait_ring_free(pe, k, ("f", r))
                nc.tensor.matmul(ring_bank(k, ("f", r))[0:96, 0:cw], aff[k][32 * q:32 * q + 32, :],
                                 yn[32 * q:32 * q + 32, 0:cw].rearrange("p (j t) -> p t j", t=T),
                                 start=True, stop=True).then_inc(s_ff[k], 1)

            def tap_weights():
                pe.wait_ge(s_gt, 2)
                for a in range(2):
                    for j in range(4):
                        ins = nc.tensor.transpose(ps[:, 2 + a, j * 128:(j + 1) * 128],
                                                  gt[:, a, j * 128:(j + 1) * 128], const("ident"))
                    ins.then_inc(s_gtm, 1)

            def decoder_weights():
                pe.wait_ge(s_wd, 1)
                for a in range(2):
                    nc.tensor.matmul(ps[:, 1, 0:C], const("mean256"), wdg[:, a, :], start=(a == 0),
                                     stop=(a == 1))
                for a in range(2):
                    ins = nc.tensor.matmul(ps[0:32, 1, 64:65], s4("wdec")[:, a * C:(a + 1) * C],
                                           s4("beta")[:, a:a + 1], start=(a == 0), stop=(a == 1))
                ins.then_inc(s_wdm, 1)

            fold("b")
            fold_constant("b")
            for k in "bg":
                n = geometry(k)[2]
                pe.wait_ge(s_ws[k], 3)
                if k == "g":
                    bias(k, 0)
                for i in range(4):
                    qk(k, i)
                if k == "b":
                    bias(k, 0)
                for i in range(4, 8):
                    qk(k, i)
                scores(k, 0)
                for i in range(8, 12):
                    qk(k, i)
                scores(k, 1)
                for i in range(12, 2 * n):
                    qk(k, i)
                scores(k, 2)
                values(k, 0)
                for c in range(chunks_of(k)):
                    transpose_pair(k, 0, c)
                values(k, 1)
                scores(k, 3)
                for g in range(4):
                    if g >= 2:
                        variance(k, g - 1)
                    for c in range(chunks_of(k)):
                        if g < 3:
                            if c == 0:
                                transpose_pair(k, g + 1, 0)
                            if c < chunks_of(k) - 1:
                                transpose_pair(k, g + 1, c + 1)
                        if g == 1 and c == 0:
                            variance(k, 0)
                        attend_pair(k, g, c)
                    if g < 2:
                        values(k, g + 2)
                    if g in (1, 2):
                        spread_rstd(k, g - 1)
                    for r in rows_of(k, g):
                        project(k, r)
                    if g == 1:
                        pe.wait_ge(s_sub[k], 8)
                        if k == "b":
                            fold("g")
                        else:
                            tap_weights()
                            decoder_weights()
                    if g in (1, 2):
                        for r in rows_of(k, g - 1):
                            feed_forward(k, r)
                    if g == 2 and k == "b":
                        fold_constant("g")
                spread_rstd(k, 2)
                variance(k, 3)
                feed_forward(k, 4)
                feed_forward(k, 5)
                spread_rstd(k, 3)
                for r in rows_of(k, 3):
                    feed_forward(k, r)

            pe.wait_ge(s_gws, 2)
            pe.wait_ge(s_wdc, 3)
            pe.wait_ge(s_first, 1)
            for n in range(NCH):
                for seg, (first, last) in enumerate(SEGMENTS):
                    if n == first:
                        pe.wait_ge(s_shhi[seg], 16 * (4 if seg else 2))
                for a in range(2):
                    i = 2 * n + a
                    if i >= 4:
                        pe.wait_ge(s_ghi, i - 3)
                    m = 0
                    for wt, ut in ((gw_hi, u4hi), (gw_lo, u4hi), (gw_hi, u4lo)):
                        for seg, (first, last) in enumerate(SEGMENTS):
                            if n == first and ut is u4lo:
                                pe.wait_ge(s_shlo[seg], 16 * 2)
                                pe.wait_ge(s_shpool[seg], 16 * 2)
                        for j in range(4):
                            at = PAD + n * CW - 4 * j
                            ins = nc.tensor.matmul(ps[:, i % 4, 0:CW], wt[:, j, a * 128:(a + 1) * 128],
                                                   ut[:, at:at + CW], start=(m == 0), stop=(m == 11))
                            m += 1
                    ins.then_inc(s_cv, 1)
            pe.wait_ge(s_wgs, 2)
            pe.wait_ge(s_we, 2)
            pe.wait_ge(s_x1, NCH)
            pe.wait_ge(s_rs["g"], 4)

            def glu(n, half, a, bank, done):
                c = slice(n * CW, (n + 1) * CW)
                o = (half * 2 + a) * 128
                m = 0
                for wt, yt in ((wglu_hi, gy_hi), (wglu_hi, gy_lo), (wglu_lo, gy_hi)):
                    for b in range(2):
                        ins = nc.tensor.matmul(ps[:, bank, 0:CW], wt[:, b, o:o + 128], yt[b][:, c],
                                               start=(m == 0), stop=(m == 5))
                        m += 1
                ins.then_inc(done, 1)

            def decode(n):
                pe.wait_ge(s_rlo, 2 * n + 2)
                if n >= 2:
                    pe.wait_ge(s_zt, n - 1)
                for q in range(TPC):
                    tok = slice(q * TT, (q + 1) * TT)
                    for a in range(2):
                        nc.tensor.matmul(decoded(n)[:, q, 0:2 * ZH], rr_hi[n % 2][a][:, tok], wdc_hl[:, a, :],
                                         start=(a == 0), stop=False, skip_group_check=True)
                        nc.tensor.matmul(decoded(n)[:, q, 0:ZH], rr_lo[n % 2][a][:, tok], wdc_hl[:, a, 0:ZH],
                                         start=False, stop=(a == 1), skip_group_check=True)
                pe.wait_ge(s_r2, n + 1)
                for q in range(TPC):
                    ins = nc.tensor.matmul(decoded(n)[:, q, 2 * ZH:ZC], rsq[n % 2][0][:, q * TT:(q + 1) * TT],
                                           const("mean256")[:, 0:1], start=True, stop=True)
                ins.then_inc(s_z, 1)

            def decoded_back(n):
                pe.wait_ge(s_zt, n + 1)
                if n >= NCH - 2:
                    pe.wait_ge(s_r, 2 * NCH)
                else:
                    pe.wait_ge(s_r, 2 * n + 5)
                for q in range(TPC):
                    ins = nc.tensor.transpose(ps[0:32, back_bank(n), q * TT:(q + 1) * TT], zt[:, n % 2, q, :],
                                              const("ident", TT)[:, 0:TT])
                ins.then_inc(s_zb, 1)

            for n in range(NCH):
                pe.wait_ge(s_glo, 2 * n + 2)
                for a in range(2):
                    i = 2 * n + a
                    if n >= 1:
                        pe.wait_ge(s_sg, i - 1)
                    elif a == 1:
                        pe.wait_ge(s_ghi, 2 * NCH)
                    glu(n, 1, a, GATE[a], s_gg)
                    if n >= 1:
                        pe.wait_ge(s_ag, i - 1)
                    glu(n, 0, a, VALUE[a], s_ga)
                    if n >= 1:
                        pe.wait_ge(s_r, i - 1)
                    elif a == 0:
                        pe.wait_ge(s_ghi, 2 * NCH - 3)
                    if n >= 3 and a == 0:
                        pe.wait_ge(s_o, n - 2)
                    nc.tensor.matmul(ps[:, ENC[a], 0:CW], wencst[:, a * 128:(a + 1) * 128],
                                     ust["s"][:, n * CW:(n + 1) * CW], start=True, stop=True).then_inc(s_gh, 1)
                if n >= 1:
                    decode(n - 1)
                if n >= 2:
                    decoded_back(n - 2)
            decode(NCH - 1)
            decoded_back(NCH - 2)
            decoded_back(NCH - 1)


def _stack(parts, rows=128):
    total = sum(a.shape[1] for a in parts)
    whole = np.zeros((rows, total), np.float32)
    at = 0
    for a in parts:
        whole[:a.shape[0], at:at + a.shape[1]] = a
        at += a.shape[1]
    return whole


def _shape_constants():
    ident = np.eye(128, dtype=np.float32)
    block = np.kron(np.eye(4), np.full((32, 32), 1 / 32)).astype(np.float32)
    center = np.tile((np.eye(32) - 1 / 32).astype(np.float32), (1, 4))
    rows = np.arange(128)
    low = [np.where(rows % 32 // HD == r, -1.0, 0.0).astype(np.float32)[:, None] for r in (2, 1)]
    return _stack([ident, block, np.full((128, 128), 1 / 256, np.float32), center,
                   np.tile(ident[:32, :32], (4, 3)), *low])


def _pick():
    n = np.arange(128)
    return (n[:, None] % 64 == n[None, :] % 64).astype(np.float16)


def _stage(qkv_w, proj_w, proj_b, ln_g, ln_b, fc1_w, fc1_b, fc2_w, fc2_b):
    qkv = qkv_w.reshape(3, HEADS, HD, C)

    def spread(w):
        out = np.zeros((C, HEADS, 4, HD), np.float32)
        out[:, :, 0:3, :] = w.transpose(2, 0, 1)[:, :, None, :]
        return np.tile(out.reshape(C, 128), (3, 1))
    return _stack([spread(qkv[0]), spread(qkv[1]), np.tile(qkv[2].reshape(C, C).T, (3, 1)), proj_w,
                   np.tile(fc1_w, (1, 4)), np.tile(fc2_w.T, (1, 3)), fc1_b[:, None],
                   np.tile(fc2_b[:, None], (3, 1)), proj_b[:, None], np.tile(ln_g[:, None], (4, 1)),
                   ln_b[:, None]])


def _halves(a):
    a = a.reshape(2, 128, -1)
    return a.transpose(1, 0, 2).reshape(128, -1)


def _table(t, side):
    w = 2 * side - 1
    t = t[:w * w].reshape(w, w, HEADS)[::-1, ::-1].transpose(2, 0, 1)
    return np.stack([t[:, :, side - 1 - x:2 * side - 1 - x] for x in range(side)]).reshape(side, HEADS, w * side)


def kernel(x, **p):
    import concourse.bacc as _bacc
    from concourse.bass_utils import run_bass_kernel_spmd as _run

    p = {k: np.asarray(v) for k, v in p.items()}
    names = ("qkv_w", "proj_w", "proj_b", "ln_g", "ln_b", "fc1_w", "fc1_b", "fc2_w", "fc2_b")
    l1 = {k[len("L1_conv_"):]: v for k, v in p.items() if k.startswith("L1_conv_")}
    arrays = {
        "x": np.asarray(x).reshape(C, C, PX // C).transpose(1, 2, 0).reshape(C, PX),
        "x_win": np.asarray(x).reshape(C, 8, 7, 8, 7).transpose(0, 1, 3, 2, 4).reshape(C, PX),
        "consts": _shape_constants(),
        "pick": _pick(),
        "stage_b": _stage(*(p["L0_conv_b_" + n] for n in names)),
        "stage_g": _stage(*(p["L0_conv_g_" + n] for n in names)),
        "s4d": _stack([np.tile(l1["W_enc"], (3, 1)), _halves(l1["W_enc"].T), _halves(l1["W_dec"]),
                       *(_halves(l1[n]) for n in ("ln_gamma", "ln_beta", "b_enc")),
                       l1["b_glu"].reshape(4, 128).T,
                       *(_halves(l1[n]) for n in ("D", "log_dt", "A_log_real", "A_imag", "C_real", "C_imag")),
                       l1["b_dec"][:, None]]),
        "w_glu": _halves(l1["W_glu"]).reshape(128, 2, 2 * DM),
        "tab_b": _table(p["L0_conv_b_rel_table"], 7),
        "tab_g": _table(p["L0_conv_g_rel_table"], 8),
    }
    arrays = {k: np.ascontiguousarray(v) for k, v in arrays.items()}
    nc = _bacc.Bacc("TRN2", target_bir_lowering=False, num_devices=1)
    args = [nc.dram_tensor(k, v.shape, mybir.dt.from_np(v.dtype), kind="ExternalInput").ap()
            for k, v in arrays.items()]
    out = nc.dram_tensor("out", (C, PX), F32, kind="ExternalOutput").ap()
    vit_s4d_kernel(nc, *args, out)
    r = _run(nc, [arrays], core_ids=[0])
    return r.results[0]["out"].reshape(1, C, IMG, IMG)
```
